# Optimizing a Trainium2 kernel written in Bass

```python
import numpy as np
import jax
import jax.numpy as jnp

def _softmax(x, axis=-1):
    return jax.nn.softmax(x, axis=axis)

def _gelu(x):
    return jax.nn.gelu(x, approximate=True)

def _silu(x):
    return jax.nn.silu(x)

def _sigmoid(x):
    return jax.nn.sigmoid(x)

def _layernorm(x, axis=-1, eps=1e-05):
    m = jnp.mean(x, axis=axis, keepdims=True)
    v = jnp.var(x, axis=axis, keepdims=True)
    return (x - m) / jnp.sqrt(v + eps)

def _scatter_add(tgt, idx, src, axis=0):
    return tgt.at[idx].add(src)

def _segment_sum(src, seg, n):
    return jax.ops.segment_sum(src, seg, n)
kernel_name = 'mk_xattn_ffn_d1_seqx_r4_e3fbae'

def setup_inputs(seed: int=0):
    np.random.seed(seed)
    _w = jnp.asarray

    def _rec_inputs():
        import jax
        import jax.numpy as jnp
        _rk = jax.random.key(seed)
        x = -1.394e-06 + 0.9999 * jax.random.normal(jax.random.fold_in(_rk, 1), (8, 100, 256), jnp.float32)
        _lenS = 100 - jax.random.randint(jax.random.fold_in(_rk, 7), (8,), 0, max(1, 100 // 4) + 1, jnp.int32)
        _lenS2 = 361 - jax.random.randint(jax.random.fold_in(_rk, 8), (8,), 0, max(1, 361 // 4) + 1, jnp.int32)
        _ctx_1024P = jax.random.normal(jax.random.fold_in(_rk, 11), (8, 16, 256), jnp.float32)
        _ctx_1024c = jax.random.dirichlet(jax.random.fold_in(_rk, 511), 0.3 * jnp.ones((16,), jnp.float32), (8, 361))
        _ctx_1024t = jnp.einsum('bsk,bkd->bsd', _ctx_1024c, _ctx_1024P)
        _ctx_1024t = _ctx_1024t * jax.lax.rsqrt(jnp.mean(jnp.square(_ctx_1024t)) + 1e-12) * 0.953939
        ctx_1024 = 7.22013e-05 + 1.00017 * (_ctx_1024t + 0.3 * jax.random.normal(jax.random.fold_in(_rk, 611), (8, 361, 256), jnp.float32))
        _validS = jnp.arange(100)[None, :] < _lenS[:, None]
        _validS2 = jnp.arange(361)[None, :] < _lenS2[:, None]
        _causal = jnp.tril(jnp.ones((100, 100), dtype=bool))
        mask_Bx1x1xS2_bk0 = jnp.logical_not(jnp.broadcast_to(_validS2[:, None, None, :], (8, 1, 1, 361)))
        return (x, ctx_1024, mask_Bx1x1xS2_bk0)
    x, ctx_1024, mask_Bx1x1xS2_bk0 = _rec_inputs()

    def _L0_xattn_setup():
        import math
        import jax, jax.numpy as jnp
        import numpy as np
        NUM_BUCKETS = 32
        MAX_DISTANCE = 128
        H = 16
        D_MODEL = 256
        D_K = D_MODEL // H

        def _relative_position_bucket(relative_position):
            nb = NUM_BUCKETS // 2
            buckets = (relative_position > 0).astype(jnp.int32) * nb
            rp = jnp.abs(relative_position)
            max_exact = nb // 2
            is_small = rp < max_exact
            rp_large = max_exact + (jnp.log(jnp.maximum(rp, 1).astype(jnp.float32) / max_exact) / math.log(MAX_DISTANCE / max_exact) * (nb - max_exact)).astype(jnp.int32)
            rp_large = jnp.minimum(rp_large, nb - 1)
            return buckets + jnp.where(is_small, rp, rp_large)
        key = jax.random.key(seed)
        ks = jax.random.split(key, 8)
        B, T_k, T_q = (4, 512, 256)
        std = D_MODEL ** (-0.5)
        inp = {'src': jax.random.normal(ks[0], (B, T_k, D_MODEL), dtype=jnp.float32), 'dst': jax.random.normal(ks[1], (B, T_q, D_MODEL), dtype=jnp.float32), 'mask': jax.random.randint(ks[2], (B, 1, 1, T_k), 0, 2).astype(bool), 'Wq': jax.random.normal(ks[3], (D_MODEL, D_MODEL), dtype=jnp.float32) * std, 'Wk': jax.random.normal(ks[4], (D_MODEL, D_MODEL), dtype=jnp.float32) * std, 'Wv': jax.random.normal(ks[5], (D_MODEL, D_MODEL), dtype=jnp.float32) * std, 'Wo': jax.random.normal(ks[6], (D_MODEL, D_MODEL), dtype=jnp.float32) * std, 'rel_bias': jax.random.normal(ks[7], (H, NUM_BUCKETS), dtype=jnp.float32) * NUM_BUCKETS ** (-0.5)}
        return inp
    _L0_xattn_all = _L0_xattn_setup()
    _L0_xattn_in = {k: v for k, v in _L0_xattn_all.items() if k in ('Wq', 'Wk', 'Wv', 'Wo', 'rel_bias')}
    del _L0_xattn_all

    def _L0_ffn_setup():
        import jax, jax.numpy as jnp
        import numpy as np
        BLOCK = 32
        W_BITS = 4
        ACT_BITS = 16

        def act_qdq(x):
            qmax = 2.0 ** (ACT_BITS - 1) - 1.0
            scale = jnp.maximum(jnp.max(jnp.abs(x)) / qmax, 1e-12)
            return jnp.clip(jnp.round(x / scale), -qmax - 1.0, qmax) * scale

        def fixed_qdq_u16(x):
            scale = 1.0 / 65536.0
            return jnp.clip(jnp.round(x / scale), 0.0, 65535.0) * scale

        def lpbq_dequant(w):
            O, I = w.shape
            qmax = 2.0 ** (W_BITS - 1) - 1.0
            wb = w.reshape(O, I // BLOCK, BLOCK)
            s = jnp.maximum(jnp.max(jnp.abs(wb), axis=-1, keepdims=True) / qmax, 1e-12)
            wq = jnp.clip(jnp.round(wb / s), -qmax - 1.0, qmax) * s
            return wq.reshape(O, I)
        key = jax.random.key(seed)
        k1, k2, k3, k4 = jax.random.split(key, 4)
        B, S, H, I = (2, 1024, 256, 768)
        x = jax.random.normal(k1, (B, S, H), jnp.float32)
        w_gate = jax.random.normal(k2, (I, H), jnp.float32) * 0.02
        w_up = jax.random.normal(k3, (I, H), jnp.float32) * 0.02
        w_down = jax.random.normal(k4, (H, I), jnp.float32) * 0.02
        return {'x': x, 'w_gate': w_gate, 'w_up': w_up, 'w_down': w_down}
    _L0_ffn_all = _L0_ffn_setup()
    _L0_ffn_in = {k: v for k, v in _L0_ffn_all.items() if k in ('w_gate', 'w_up', 'w_down')}
    del _L0_ffn_all
    return {'x': x, 'ctx_1024': ctx_1024, 'mask_Bx1x1xS2_bk0': mask_Bx1x1xS2_bk0, 'L0_xattn_Wq': _L0_xattn_in['Wq'], 'L0_xattn_Wk': _L0_xattn_in['Wk'], 'L0_xattn_Wv': _L0_xattn_in['Wv'], 'L0_xattn_Wo': _L0_xattn_in['Wo'], 'L0_xattn_rel_bias': _L0_xattn_in['rel_bias'], 'L0_ffn_w_gate': _L0_ffn_in['w_gate'], 'L0_ffn_w_up': _L0_ffn_in['w_up'], 'L0_ffn_w_down': _L0_ffn_in['w_down']}

def reference(x, ctx_1024, mask_Bx1x1xS2_bk0, L0_xattn_Wq, L0_xattn_Wk, L0_xattn_Wv, L0_xattn_Wo, L0_xattn_rel_bias, L0_ffn_w_gate, L0_ffn_w_up, L0_ffn_w_down):
    import jax
    import jax.numpy as jnp

    def _L0_xattn_ref(src, dst, mask, Wq, Wk, Wv, Wo, rel_bias):
        import math
        import jax, jax.numpy as jnp
        import numpy as np
        NUM_BUCKETS = 32
        MAX_DISTANCE = 128
        H = 16
        D_MODEL = 256
        D_K = D_MODEL // H

        def _relative_position_bucket(relative_position):
            nb = NUM_BUCKETS // 2
            buckets = (relative_position > 0).astype(jnp.int32) * nb
            rp = jnp.abs(relative_position)
            max_exact = nb // 2
            is_small = rp < max_exact
            rp_large = max_exact + (jnp.log(jnp.maximum(rp, 1).astype(jnp.float32) / max_exact) / math.log(MAX_DISTANCE / max_exact) * (nb - max_exact)).astype(jnp.int32)
            rp_large = jnp.minimum(rp_large, nb - 1)
            return buckets + jnp.where(is_small, rp, rp_large)
        B, T_k, _ = src.shape
        T_q = dst.shape[1]
        q = (dst @ Wq.T).reshape(B, T_q, H, D_K)
        k = (src @ Wk.T).reshape(B, T_k, H, D_K)
        v = (src @ Wv.T).reshape(B, T_k, H, D_K)
        scores = jnp.einsum('bqhd,bkhd->bhqk', q, k)
        rel_pos = jnp.arange(T_k)[None, :] - jnp.arange(T_q)[:, None]
        rp_bucket = _relative_position_bucket(rel_pos)
        bias = rel_bias[:, rp_bucket]
        scores = scores + bias[None]
        scores = jnp.where(mask, scores, -1000000000.0)
        attn = jax.nn.softmax(scores, axis=-1)
        out = jnp.einsum('bhqk,bkhd->bqhd', attn, v).reshape(B, T_q, H * D_K)
        return out @ Wo.T

    def _L0_ffn_ref(x, w_gate, w_up, w_down):
        import jax, jax.numpy as jnp
        import numpy as np
        BLOCK = 32
        W_BITS = 4
        ACT_BITS = 16

        def act_qdq(x):
            qmax = 2.0 ** (ACT_BITS - 1) - 1.0
            scale = jnp.maximum(jnp.max(jnp.abs(x)) / qmax, 1e-12)
            return jnp.clip(jnp.round(x / scale), -qmax - 1.0, qmax) * scale

        def fixed_qdq_u16(x):
            scale = 1.0 / 65536.0
            return jnp.clip(jnp.round(x / scale), 0.0, 65535.0) * scale

        def lpbq_dequant(w):
            O, I = w.shape
            qmax = 2.0 ** (W_BITS - 1) - 1.0
            wb = w.reshape(O, I // BLOCK, BLOCK)
            s = jnp.maximum(jnp.max(jnp.abs(wb), axis=-1, keepdims=True) / qmax, 1e-12)
            wq = jnp.clip(jnp.round(wb / s), -qmax - 1.0, qmax) * s
            return wq.reshape(O, I)
        x = act_qdq(x)
        up = act_qdq(x @ lpbq_dequant(w_up).T)
        gate = act_qdq(x @ lpbq_dequant(w_gate).T)
        sig = fixed_qdq_u16(jax.nn.sigmoid(gate))
        gate = act_qdq(gate * sig)
        o = act_qdq(gate * up)
        return o @ lpbq_dequant(w_down).T
    x = x + _L0_xattn_ref(ctx_1024, _layernorm(x, axis=-1), mask_Bx1x1xS2_bk0, L0_xattn_Wq, L0_xattn_Wk, L0_xattn_Wv, L0_xattn_Wo, L0_xattn_rel_bias)
    x = x + _L0_ffn_ref(_layernorm(x, axis=-1), L0_ffn_w_gate, L0_ffn_w_up, L0_ffn_w_down)
    return x

_drawn_inputs = setup_inputs


def setup_inputs(seed=0):
    import zlib

    import numpy as np

    out = dict(_drawn_inputs(seed))
    spreads = {}
    factors = {}
    for name, (base, spread) in spreads.items():
        noise = np.random.default_rng([zlib.crc32(name.encode()), seed]).standard_normal(out[name].shape)
        drawn = base * np.exp(spread * noise) if base else spread * noise
        out[name] = jnp.asarray(drawn.astype(out[name].dtype))
    for name, factor in factors.items():
        out[name] = (out[name] * factor).astype(out[name].dtype)
    return out
```

```python
from contextlib import ExitStack

import numpy as np

import concourse.bass as bass
from concourse import mybir

ALU = mybir.AluOpType
ACT = mybir.ActivationFunctionType
AX = mybir.AxisListType
F32 = mybir.dt.float32
F32R = mybir.dt.float32r
BF16 = mybir.dt.bfloat16
I16 = mybir.dt.int16
U16 = mybir.dt.uint16
U8 = mybir.dt.uint8
RMAX = bass.bass_isa.ReduceOp.max

P = 128
B, TQ, TK, DM = 8, 100, 361, 256
H, DK = 16, 16
GH = 4
NG = H // GH
NI = B * NG
NH = NI * GH
KC = DM // P
NT = 3
KT = (TK + NT - 1) // NT
TKE = TK + TK % 2
VW = DK + 1
NTOK = B * TQ
HALF = NTOK // 2
FF = 768
FC = FF // P
WBLK = 32
NREL = TQ + TK - 1
NBUCKET = 32
MASKED = float(2.0 ** 100)
LN_EPS = 1e-5
PRODUCTS = [(0, 0), (0, 1), (1, 0)]
ACT_QMAX = 32767.0
W_QMAX = 7.0
MIN_SCALE = 1e-12
UBITS = 65536.0
ROUND = 1.5 * 2.0 ** 23

FAR_FROM = [8, 12, 16, 23, 32, 46, 64, 91]


def bucket_of(rel):
    dist = abs(rel)
    bucket = dist if dist < 8 else 7 + sum(dist >= d for d in FAR_FROM)
    return bucket + (NBUCKET // 2 if rel > 0 else 0)


def build(nc, x, ctxT, mask, wqT, wkT, wvT, woT, relT, w_gate, w_up, w_down, onehot, hmask, ident, out):
    rel_row = nc.dram_tensor("rel_row", [H, NREL], F32, kind="Internal")

    with ExitStack() as ctx:
        def sb(name, shape, dt=F32):
            return ctx.enter_context(nc.sbuf_tensor(name, shape, dt))

        def sem(name):
            return ctx.enter_context(nc.semaphore(name))

        bank = [ctx.enter_context(nc.psum_tensor(f"bank{n}", [P, 512], F32)) for n in range(8)]

        x_sb = sb("x_sb", [TQ, B, DM])
        region_ctx = sb("region_ctx", [P, KC * (B * TK + 2)])
        region_bias = sb("region_bias", [P, H * TK])
        region_v = sb("region_v", [P, NI * NT * GH * VW])
        region_ffw = sb("region_ffw", [P, 3 * FC * DM])
        ctxT_sb = region_ctx[:].rearrange("p (c n) -> p c n", c=KC)
        wq_sb = sb("wq_sb", [P, KC, NG, P])
        wk_sb = sb("wk_sb", [P, KC, DM])
        wv_sb = sb("wv_sb", [P, KC, DM])
        wo_sb = sb("wo_sb", [P, KC, DM])
        rel_sb = sb("rel_sb", [NBUCKET, H])
        onehot_sb = region_bias[0:NBUCKET, 0:NREL]
        hmask_sb = sb("hmask_sb", [P, GH])
        ident_sb = sb("ident_sb", [P, P])
        mask_u8 = region_v[0:TQ, 0:B * TK // 4].bitcast(U8)
        ffw = region_ffw[:].rearrange("p (m n) -> p m n", m=3)
        relrow_sb = region_bias[0:H, NREL:2 * NREL]
        bias_sb = region_bias[0:TQ, :].rearrange("p (h n) -> p h n", h=H)
        mask_add = sb("mask_add", [TQ, B, TK], BF16)
        xn = sb("xn", [TQ, B, DM])
        attn = xn[:].rearrange("p b (g n) -> p (b g) n", g=NG)
        xT = sb("xT", [P, KC, NTOK])
        region_q = sb("region_q", [P, 2 * NI * TQ], F32R)
        region_k = sb("region_k", [P, NI * TKE], F32R)
        qh, ql = (region_q[:, m * NI * TQ:(m + 1) * NI * TQ].rearrange("p (i n) -> p i n", i=NI) for m in range(2))
        kst = region_k[:].rearrange("p (i n) -> p i n", i=NI)
        v_sb = region_v[0:KT, :].rearrange("p (i t h w) -> p i t h w", i=NI, t=NT, h=GH)
        qm = sb("qm", [P, 2, 2, GH, TQ], F32R)
        mbias = region_ctx[0:TQ, 0:2 * GH * TK].rearrange("p (u h n) -> p u h n", u=2, h=GH)
        at = 2 * GH * TK
        prob = region_ctx[0:TQ, at:at + 4 * NT * KT].rearrange("p (s n) -> p s n", s=4)
        nmax = sb("nmax", [TQ, 4])
        at += 4 * NT * KT
        pT = region_ctx[0:KT, at:at + 4 * NT * TQ].rearrange("p (s n) -> p s n", s=4)
        rden = sb("rden", [TQ, 2, GH])
        stats = sb("stats", [TQ, B, 6])
        mv = sb("mv", [TQ, B, 2])
        veps = sb("veps", [TQ, B])
        rstd = sb("rstd", [TQ, B])
        mhalf = sb("mhalf", [TQ, B])
        wmax = sb("wmax", [P, 3, FC * DM // WBLK])
        wscale = sb("wscale", [P, 3, FC * DM // WBLK])
        winv = sb("winv", [P, 3, FC * DM // WBLK])
        part = sb("part", [P, 5, 2 * FC])
        amax = sb("amax", [P, 5])
        gmax = sb("gmax", [P, 5])
        scl = sb("scl", [P, 5, 4])
        wT = region_k[:, 0:6 * FC * DM].rearrange("p (m s n) -> p m s n", m=3, s=2)
        xq = region_q[:, 0:2 * KC * NTOK].rearrange("p (s k n) -> p s k n", s=2, k=KC)
        oq = [t[:, 0:FC * NTOK].rearrange("p (k n) -> p k n", k=FC) for t in (region_q, region_k)]
        gate, up = (t[:, 0:FC * NTOK].rearrange("p (c n) -> p c n", c=FC) for t in (region_ctx, region_bias))
        x_int = region_ffw[:, FC * NTOK // 2:(FC + KC) * NTOK // 2].bitcast(I16).rearrange("p (c n) -> p c n", c=KC)
        g_int, u_int = (region_v[:, m * FC * NTOK // 2:(m + 1) * FC * NTOK // 2].bitcast(I16).rearrange("p (c n) -> p c n", c=FC)
                        for m in range(2))
        s_int = region_ffw[:, 0:FC * NTOK // 2].bitcast(U16).rearrange("p (c n) -> p c n", c=FC)

        loaded = {n: sem(f"loaded_{n}") for n in ("x", "ctx", "wq", "wk", "wv", "wo", "const", "mask", "ffw")}
        relrow_stored, bias_loaded, out_stored = sem("relrow_stored"), sem("bias_loaded"), sem("out_stored")
        dve_step, pool_step = sem("dve_step"), sem("pool_step")
        ln_var, ln_rstd, xn_done = sem("ln_var"), sem("ln_rstd"), sem("xn_done")
        wmax_done, ffw_done, fill_done, mask_done = sem("wmax_done"), sem("ffw_done"), sem("fill_done"), sem("mask_done")
        pad_done, ones_done = sem("pad_done"), sem("ones_done")
        job_done, act_evac, dve_evac = sem("job_done"), sem("act_evac"), sem("dve_evac")
        qm_ready, bias_ready = sem("qm_ready"), sem("bias_ready")
        scores_ready, z_done, prob_ready, t_ready = sem("scores_ready"), sem("z_done"), sem("prob_ready"), sem("t_ready")
        pt_even, pt_odd = sem("pt_even"), sem("pt_odd")
        o_ready, rden_done, attn_done = sem("o_ready"), sem("rden_done"), sem("attn_done")
        tail_pe, tail_act, tail_dve = sem("tail_pe"), sem("tail_act"), sem("tail_dve")
        amax_ready, gmax_ready, scale_ready = sem("amax_ready"), sem("gmax_ready"), sem("scale_ready")
        sig_ready, sint_ready = sem("sig_ready"), sem("sint_ready")

        jobs = ([("rel", 0, 0)] + [("xT", c, 0) for c in range(B // 2)]
                + [("q", g, hf) for g in range(NG) for hf in range(2)]
                + [("k", b, m) for b in range(B) for m in range(KC)]
                + [("v", b, t) for b in range(B) for t in range(NT)])
        on_act = [kind in ("rel", "xT", "q", "k") or (kind == "v" and t % 2 == 0) for kind, _, t in jobs]
        on_dve = [kind in ("q", "k") or (kind == "v" and t % 2 == 1) for kind, _, t in jobs]

        def act_after(n):
            return sum(on_act[:n + 1])

        def dve_after(n):
            return sum(on_dve[:n + 1])

        def bank_free(eng, n):
            if n >= 8:
                if on_act[n - 8]:
                    eng.wait_ge(act_evac, act_after(n - 8))
                if on_dve[n - 8]:
                    eng.wait_ge(dve_evac, dve_after(n - 8))

        first_job = {}
        last_job = {}
        for n, (kind, _, _) in enumerate(jobs):
            first_job.setdefault(kind, n)
            last_job[kind] = n

        P_AT = 9 + B // 2
        P_WO, P_XT, P_GU = P_AT + B // 2, P_AT + B, P_AT + B + 4 * FC
        A_GU = 9 + B // 2 + B // 2
        T_RES = 9 + B // 2
        T_XT = T_RES + 1
        T_O = T_XT + 1
        T_OUT = T_O

        block = ctx.enter_context(nc.Block())

        @block.sync
        def _(sp):
            sp.dma_start(x_sb[:], x.rearrange("b q d -> q b d")).then_inc(loaded["x"], 16)
            sp.dma_start(onehot_sb[:], onehot).then_inc(loaded["const"], 16)
            sp.dma_start(rel_sb[:], relT).then_inc(loaded["const"], 16)
            sp.dma_start(ident_sb[:], ident).then_inc(loaded["const"], 16)
            sp.dma_start(hmask_sb[:], hmask).then_inc(loaded["const"], 16)
            sp.dma_start(wq_sb[:], wqT.rearrange("(c p) g m -> p c g m", p=P)).then_inc(loaded["wq"], 16)
            sp.dma_start(wk_sb[:], wkT.rearrange("(c p) m -> p c m", p=P)).then_inc(loaded["wk"], 16)
            cols = ctxT.rearrange("(c p) n -> p c n", p=P)
            for n in range(4):
                w = 2 * TK
                sp.dma_start(ctxT_sb[:, :, n * w:(n + 1) * w], cols[:, :, n * w:(n + 1) * w]).then_inc(loaded["ctx"], 16)
                sp.wait_ge(loaded["ctx"], 16 * (n + 1))
            sp.dma_start(wv_sb[:], wvT.rearrange("(c p) m -> p c m", p=P)).then_inc(loaded["wv"], 16)
            sp.dma_start(wo_sb[:], woT.rearrange("(c p) m -> p c m", p=P)).then_inc(loaded["wo"], 16)
            sp.wait_ge(act_evac, act_after(first_job["rel"]))
            sp.dma_start(rel_row.ap(), relrow_sb[:]).then_inc(relrow_stored, 16)
            sp.wait_ge(relrow_stored, 16)
            window = bass.AP(rel_row, 0, [[1, TQ], [NREL, H], [1, TK]])
            sp.dma_start(bias_sb[:], window).then_inc(bias_loaded, 16)
            for c in range(B // 2):
                sp.wait_ge(tail_dve, T_OUT + c + 1)
                sp.dma_start(out[2 * c:2 * c + 2].rearrange("b q d -> q b d"), x_sb[:, 2 * c:2 * c + 2, :]).then_inc(out_stored, 16)
            sp.wait_ge(out_stored, 16 * (B // 2))

        @block.gpsimd
        def _(pool):
            steps = [0]

            def link(ins):
                steps[0] += 1
                ins.then_inc(pool_step, 1)
                pool.wait_ge(pool_step, steps[0])

            pool.dma_start(ffw[:, 0, :].rearrange("p (c i) -> p c i", c=FC),
                           w_gate.rearrange("(c p) i -> p c i", p=P)).then_inc(loaded["ffw"], 16)
            pool.dma_start(ffw[:, 1, :].rearrange("p (c i) -> p c i", c=FC),
                           w_up.rearrange("(c p) i -> p c i", p=P)).then_inc(loaded["ffw"], 16)
            pool.dma_start(ffw[:, 2, :].rearrange("p (c i) -> p c i", c=KC),
                           w_down.rearrange("(c p) i -> p c i", p=P)).then_inc(loaded["ffw"], 16)
            pool.dma_start(mask_u8, mask.rearrange("b n -> (b n)").partition_broadcast(TQ)).then_inc(loaded["mask"], 16)
            nc.gpsimd.memset(mhalf[:], -0.5).then_inc(fill_done, 1)
            nc.gpsimd.memset(ctxT_sb[:, :, B * TK:], 0.0).then_inc(fill_done, 1)
            nc.gpsimd.memset(kst[:, :, TK:].bitcast(F32), 0.0).then_inc(fill_done, 1)
            nc.gpsimd.memset(amax[:], 0.0).then_inc(fill_done, 1)

            def rsqrt_of_var(n):
                pool.wait_ge(ln_var, n)
                link(nc.gpsimd.tensor_scalar(veps[:], mv[:, :, 1], LN_EPS, None, ALU.add))
                nc.gpsimd.tensor_tensor(rstd[:], veps[:], mhalf[:], ALU.pow).then_inc(ln_rstd, 1)

            rsqrt_of_var(1)

            pool.wait_ge(loaded["mask"], 16)
            nc.gpsimd.tensor_scalar(mask_add[:].rearrange("p b n -> p (b n)"), mask_u8, -1.0, MASKED,
                                    ALU.add, ALU.mult).then_inc(mask_done, 1)
            pool.wait_ge(mask_done, 1)
            nc.gpsimd.memset(v_sb[:, :, :, :, DK:], 1.0).then_inc(ones_done, 1)

            def prepare(b, g, i):
                u = g % 2
                pool.wait_ge(loaded["const"], 64)
                if not (isinstance(i, int) and i < 2):
                    pool.wait_ge(scores_ready, i * GH - GH)
                for part_no, src in ((0, qh), (1, ql)):
                    ins = nc.gpsimd.tensor_tensor(
                        qm[:, u, part_no], src[:, bass.ds(i, 1), :].bitcast(F32).to_broadcast([P, GH, TQ]),
                        hmask_sb[:].unsqueeze(2).to_broadcast([P, GH, TQ]), ALU.mult)
                ins.then_inc(qm_ready, 1)
                pool.wait_ge(mask_done, 1)
                if not (isinstance(i, int) and i < 2):
                    pool.wait_ge(z_done, i * GH - GH)
                nc.gpsimd.tensor_tensor(
                    mbias[:, u], bias_sb[:, g * GH:(g + 1) * GH, :],
                    mask_add[:, bass.ds(b, 1), :].to_broadcast([TQ, GH, TK]), ALU.add).then_inc(bias_ready, 1)

            for m in range(3):
                w = ffw[:, m, :].rearrange("p (n k) -> p n k", k=WBLK)
                pool.wait_ge(wmax_done, m + 1)
                link(nc.gpsimd.tensor_tensor(w, w, winv[:, m, :].unsqueeze(2).to_broadcast([P, FC * DM // WBLK, WBLK]), ALU.mult))
                link(nc.gpsimd.tensor_scalar(w, w, ROUND, -ROUND, ALU.add, ALU.add))
                link(nc.gpsimd.tensor_scalar(w, w, W_QMAX, -W_QMAX - 1.0, ALU.min, ALU.max))
                nc.gpsimd.tensor_tensor(w, w, wscale[:, m, :].unsqueeze(2).to_broadcast([P, FC * DM // WBLK, WBLK]),
                                        ALU.mult).then_inc(ffw_done, 1)

            pool.wait_ge(act_evac, act_after(last_job["q"]))
            pool.wait_ge(dve_evac, dve_after(last_job["q"]))
            pool.wait_ge(loaded["const"], 64)
            pool.wait_ge(bias_loaded, 16)
            pool.wait_ge(job_done, len(jobs))
            nc.gpsimd.memset(prob[:, :, TK:], 0.0).then_inc(pad_done, 1)
            for g in range(NG):
                prepare(0, g, g)
            with nc.gpsimd.Fori(1, B) as b:
                for g in range(NG):
                    prepare(b, g, b * NG + g)

            rsqrt_of_var(2)
            for n in range(5):
                pool.wait_ge(amax_ready, n + 1)
                nc.gpsimd.partition_all_reduce(gmax[:, n:n + 1], amax[:, n:n + 1], P, RMAX).then_inc(gmax_ready, 1)

        @block.tensor
        def _(pe):
            pe.wait_ge(loaded["const"], 64)
            pe.wait_ge(fill_done, 4)
            ctx_seen = 0
            for n, (kind, a, c) in enumerate(jobs):
                bk = bank[n % 8]
                bank_free(pe, n)
                if kind == "rel":
                    mm = nc.tensor.matmul(bk[0:H, 0:NREL], rel_sb[:], onehot_sb[:], start=True, stop=True)
                elif kind == "xT":
                    pe.wait_ge(xn_done, a + 1)
                    for j in range(2):
                        for k in range(KC):
                            mm = nc.tensor.transpose(bk[:, (2 * k + j) * TQ:(2 * k + j + 1) * TQ],
                                                     xn[:, 2 * a + j, k * P:(k + 1) * P], ident_sb[0:TQ, 0:TQ])
                elif kind == "q":
                    if n == first_job["q"]:
                        pe.wait_ge(loaded["wq"], 16)
                        pe.wait_ge(act_evac, act_after(last_job["xT"]))
                    for k in range(KC):
                        mm = nc.tensor.matmul(bk[:, 0:HALF], wq_sb[:, k, a, :], xT[:, k, c * HALF:(c + 1) * HALF],
                                              start=(k == 0), stop=(k == KC - 1))
                elif kind == "k":
                    if n == first_job["k"]:
                        pe.wait_ge(loaded["wk"], 16)
                    if a // 2 + 1 > ctx_seen:
                        ctx_seen = a // 2 + 1
                        pe.wait_ge(loaded["ctx"], 16 * ctx_seen)
                    for k in range(KC):
                        mm = nc.tensor.matmul(bk[:, 0:TK], wk_sb[:, k, c * P:(c + 1) * P],
                                              ctxT_sb[:, k, a * TK:(a + 1) * TK], start=(k == 0), stop=(k == KC - 1))
                elif kind == "v":
                    if n == first_job["v"]:
                        pe.wait_ge(loaded["wv"], 16)
                        pe.wait_ge(ones_done, 1)
                    s = a * TK + c * KT
                    for k in range(KC):
                        mm = nc.tensor.matmul(bk[0:KT, 0:DM], ctxT_sb[:, k, s:s + KT], wv_sb[:, k, :],
                                              start=(k == 0), stop=(k == KC - 1))
                mm.then_inc(job_done, 1)

            pe.wait_ge(act_evac, act_after(len(jobs) - 1))
            pe.wait_ge(dve_evac, dve_after(len(jobs) - 1))

            def scores(step2, j, m, i, first):
                bk = bank[j % 4]
                u = (j // GH) % 2
                if j % GH == 0:
                    pe.wait_ge(qm_ready, i + 1)
                if not first:
                    pe.wait_ge(z_done, m - 3)
                for part_no in range(2):
                    mm = nc.tensor.matmul(bk[0:TQ, 0:TKE], qm[:, u, part_no, j % GH, :],
                                          kst[:, bass.ds(i, 1), :].rearrange("p a n -> p (a n)"),
                                          start=(part_no == 0), stop=(part_no == 1))
                mm.then_inc(scores_ready, 1)

            def weigh(p, j):
                n = p * 8 + j
                i = p * 2 + j // GH
                u = (j // GH) % 2
                bk = bank[6 + u]
                pe.wait_ge(pt_even if j % 2 == 0 else pt_odd, p * 4 + j // 2 + 1)
                if j % GH == 0 and not (isinstance(i, int) and i < 2):
                    pe.wait_ge(attn_done, i - 1)
                h = j % GH
                for t in range(NT):
                    mm = nc.tensor.matmul(bk[0:TQ, h * VW:(h + 1) * VW], pT[:, j % 4, t * TQ:(t + 1) * TQ],
                                          v_sb[:, bass.ds(i, 1), t, h, :].rearrange("p a n -> p (a n)"),
                                          start=(t == 0), stop=(t == NT - 1))
                mm.then_inc(o_ready, 1)

            def two_steps(p, last):
                static = isinstance(p, int)
                for j in range(8):
                    if not (last and j + 3 >= 8):
                        m = p * 8 + (j + 3)
                        jj = (j + 3) % 8
                        scores(None, jj, m, p * 2 + (j + 3) // GH, static and m < 4)
                    n = p * 8 + j
                    bk = bank[4 + j % 2]
                    pe.wait_ge(prob_ready, n + 1)
                    if not (static and n < 2):
                        pe.wait_ge(pt_even if j % 2 == 0 else pt_odd, p * 4 + j // 2)
                    for t in range(NT):
                        mm = nc.tensor.transpose(bk[0:KT, t * TQ:(t + 1) * TQ], prob[:, j % 4, t * KT:(t + 1) * KT],
                                                 ident_sb[0:TQ, 0:TQ])
                    mm.then_inc(t_ready, 1)
                    if j > 0:
                        weigh(p, j - 1)
                    elif not (static and p == 0):
                        weigh(p - 1, 7)

            pe.wait_ge(pad_done, 1)
            for m in range(3):
                scores(None, m, m, 0, True)
            two_steps(0, False)
            with nc.tensor.Fori(1, NI // 2 - 1) as p:
                two_steps(p, False)
            two_steps(NI // 2 - 1, True)
            weigh(NI // 2 - 1, 7)

            pe.wait_ge(ffw_done, 3)
            pe.wait_ge(z_done, NH)
            pe.wait_ge(pt_even, NH // 2)
            pe.wait_ge(pt_odd, NH // 2)
            pe.wait_ge(attn_done, NI)
            for r in range(9):
                m, c = r // 3, r % 3
                if r >= 8:
                    pe.wait_ge(tail_dve, r - 7)
                for j in range(4):
                    t = 4 * c + j
                    at = (t % FC) * DM + (t // FC) * P if m < 2 else (t % KC) * FF + (t // KC) * P
                    mm = nc.tensor.transpose(bank[r % 8][:, j * P:(j + 1) * P], ffw[:, m, at:at + P], ident_sb[:])
                mm.then_inc(tail_pe, 1)
            pe.wait_ge(loaded["wo"], 16)
            pe.wait_ge(tail_dve, 9)
            for c in range(B // 2):
                for j in range(2):
                    for k in range(KC):
                        mm = nc.tensor.transpose(bank[c][:, (2 * k + j) * TQ:(2 * k + j + 1) * TQ],
                                                 attn[:, (2 * c + j) * NG:(2 * c + j + 1) * NG, :].rearrange("p a n -> p (a n)")[:, k * P:(k + 1) * P],
                                                 ident_sb[0:TQ, 0:TQ])
                mm.then_inc(tail_pe, 1)
            for c in range(B // 2):
                pe.wait_ge(tail_act, 9 + c + 1)
                for j in range(2):
                    for k in range(KC):
                        mm = nc.tensor.matmul(bank[4 + c][0:TQ, j * DM:(j + 1) * DM], xT[:, k, (2 * c + j) * TQ:(2 * c + j + 1) * TQ],
                                              wo_sb[:, k, :], start=(k == 0), stop=(k == KC - 1))
                mm.then_inc(tail_pe, 1)
            for c in range(B // 2):
                pe.wait_ge(xn_done, B // 2 + c + 1)
                for j in range(2):
                    for k in range(KC):
                        mm = nc.tensor.transpose(bank[c][:, (2 * k + j) * TQ:(2 * k + j + 1) * TQ],
                                                 xn[:, 2 * c + j, k * P:(k + 1) * P], ident_sb[0:TQ, 0:TQ])
                mm.then_inc(tail_pe, 1)
            pe.wait_ge(tail_dve, T_XT)
            for r in range(4 * FC):
                m, fc, hf = r // (2 * FC), r // 2 % FC, r % 2
                pe.wait_ge(tail_act, A_GU + max(r - 7, 0))
                for k in range(KC):
                    for ws, xs in PRODUCTS:
                        mm = nc.tensor.matmul(bank[r % 8][:, 0:HALF], wT[:, m, ws, k * FF + fc * P:k * FF + (fc + 1) * P],
                                              xq[:, xs, k, hf * HALF:(hf + 1) * HALF], start=(k == 0 and (ws, xs) == PRODUCTS[0]),
                                              stop=(k == KC - 1 and (ws, xs) == PRODUCTS[-1]))
                mm.then_inc(tail_pe, 1)
            pe.wait_ge(tail_act, A_GU + 4 * FC)
            for c in range(B // 2):
                pe.wait_ge(tail_dve, T_O)
                for j in range(2):
                    for k in range(FC):
                        for ws, xs in PRODUCTS:
                            mm = nc.tensor.matmul(bank[c][0:TQ, j * DM:(j + 1) * DM], oq[xs][:, k, (2 * c + j) * TQ:(2 * c + j + 1) * TQ],
                                                  wT[:, 2, ws, k * DM:(k + 1) * DM], start=(k == 0 and (ws, xs) == PRODUCTS[0]),
                                                  stop=(k == FC - 1 and (ws, xs) == PRODUCTS[-1]))
                mm.then_inc(tail_pe, 1)

        @block.scalar
        def _(act):
            for n, (kind, a, c) in enumerate(jobs):
                if not on_act[n]:
                    continue
                bk = bank[n % 8]
                act.wait_ge(job_done, n + 1)
                if kind == "rel":
                    ins = nc.scalar.copy(relrow_sb[:], bk[0:H, 0:NREL])
                elif kind == "xT":
                    ins = nc.scalar.copy(xT[:, :, 2 * a * TQ:2 * (a + 1) * TQ],
                                         bk[:, 0:4 * TQ].rearrange("p (k n) -> p k n", k=KC))
                elif kind == "q":
                    ins = nc.scalar.copy(
                        qh[:].rearrange("p (b g) q -> p b g q", g=NG)[:, c * B // 2:(c + 1) * B // 2, a, :],
                        bk[:, 0:HALF].rearrange("p (b q) -> p b q", q=TQ))
                elif kind == "k":
                    nc.scalar.copy(kst[0:64, a * NG + 2 * c, 0:TK], bk[0:64, 0:TK])
                    ins = nc.scalar.copy(kst[64:P, a * NG + 2 * c + 1, 0:TK], bk[64:P, 0:TK])
                else:
                    ins = nc.scalar.copy(v_sb[:, a * NG:(a + 1) * NG, c, :, 0:DK],
                                         bk[0:KT, 0:DM].rearrange("p (g h d) -> p g h d", g=NG, h=GH))
                ins.then_inc(act_evac, 1)

            def exponent(p, j, m):
                act.wait_ge(z_done, m + 1)
                nc.scalar.activation(prob[:, j % 4, 0:TK], prob[:, j % 4, 0:TK], ACT.Exp, bias=nmax[:, j % 4:j % 4 + 1],
                                     scale=-1.0).then_inc(prob_ready, 1)

            def two_steps(p, last):
                for j in range(8):
                    n = p * 8 + j
                    if not (last and j == 7):
                        exponent(p, (j + 1) % 8, n + 1)
                    if j % 2 == 0:
                        act.wait_ge(t_ready, n + 1)
                        if not (isinstance(n, int) and n < 4):
                            act.wait_ge(o_ready, n - 3)
                        nc.scalar.copy(pT[:, j % 4, :], bank[4 + j % 2][0:KT, 0:NT * TQ]).then_inc(pt_even, 1)

            exponent(0, 0, 0)
            two_steps(0, False)
            with nc.scalar.Fori(1, NI // 2 - 1) as p:
                two_steps(p, False)
            two_steps(NI // 2 - 1, True)

            for r in range(9):
                act.wait_ge(tail_pe, r + 1)
                nc.scalar.copy(wT[:, r // 3, 0, r % 3 * 512:(r % 3 + 1) * 512], bank[r % 8][:]).then_inc(tail_act, 1)
            for c in range(B // 2):
                act.wait_ge(tail_pe, 9 + c + 1)
                nc.scalar.copy(xT[:, :, 2 * c * TQ:2 * (c + 1) * TQ],
                               bank[c][:, 0:4 * TQ].rearrange("p (k n) -> p k n", k=KC)).then_inc(tail_act, 1)
            act.wait_ge(tail_pe, P_XT)
            act.wait_ge(scale_ready, 1)
            for c in range(B // 2):
                nc.scalar.activation(x_int[:, :, 2 * c * TQ:2 * (c + 1) * TQ],
                                     bank[c][:, 0:4 * TQ].rearrange("p (k n) -> p k n", k=KC),
                                     ACT.Copy, scale=scl[:, 0, 2:3]).then_inc(tail_act, 1)

            def gate_up(r):
                m, fc, hf = r // (2 * FC), r // 2 % FC, r % 2
                act.wait_ge(tail_pe, P_XT + r + 1)
                nc.scalar.copy((gate, up)[m][:, fc, hf * HALF:(hf + 1) * HALF], bank[r % 8][:, 0:HALF]).then_inc(tail_act, 1)

            for r in range(4 * FC):
                gate_up(r)
            act.wait_ge(scale_ready, 2)
            for fc in range(FC):
                act.wait_ge(sint_ready, fc + 1)
                nc.scalar.activation(gate[:, fc, :], g_int[:, fc, :], ACT.Sigmoid,
                                     scale=scl[:, 1, 1:2]).then_inc(sig_ready, 1)

        @block.vector
        def _(dve):
            steps = [0]

            def link(ins):
                steps[0] += 1
                ins.then_inc(dve_step, 1)
                dve.wait_ge(dve_step, steps[0])

            def layer_norm(rep):
                for b in range(B):
                    if rep:
                        if b % 2 == 0:
                            dve.wait_ge(tail_pe, P_AT + b // 2 + 1)
                            link(nc.vector.tensor_tensor(x_sb[:, b:b + 2, :], bank[4 + b // 2][0:TQ, :].rearrange("p (j d) -> p j d", j=2),
                                                         x_sb[:, b:b + 2, :], ALU.add))
                            dve.sem_inc(tail_dve, 1)
                    ins = nc.vector.bn_stats(stats[:, b, :], x_sb[:, b, :])
                link(ins)
                for b in range(B):
                    ins = nc.vector.bn_aggr(mv[:, b, :], stats[:, b, :])
                ins.then_inc(ln_var, 1)
                dve.wait_ge(ln_rstd, rep + 1)
                for b in range(B):
                    ins = nc.vector.tensor_scalar(xn[:, b, :], x_sb[:, b, :], mv[:, b, 0:1], rstd[:, b:b + 1],
                                                  ALU.subtract, ALU.mult)
                    if b % 2 == 1:
                        ins.then_inc(xn_done, 1)

            dve.wait_ge(loaded["x"], 16)
            layer_norm(0)

            dve.wait_ge(loaded["ffw"], 48)
            for m in range(3):
                w = ffw[:, m, :].rearrange("p (n k) -> p n k", k=WBLK)
                link(nc.vector.tensor_reduce(wmax[:, m, :], w, AX.X, ALU.max, apply_absolute_value=True))
                link(nc.vector.tensor_scalar(wscale[:, m, :], wmax[:, m, :], 1.0 / W_QMAX, MIN_SCALE, ALU.mult, ALU.max))
                nc.vector.reciprocal(winv[:, m, :], wscale[:, m, :]).then_inc(wmax_done, 1)

            for n, (kind, a, c) in enumerate(jobs):
                if not on_dve[n]:
                    continue
                bk = bank[n % 8]
                if on_act[n]:
                    dve.wait_ge(act_evac, act_after(n))
                else:
                    dve.wait_ge(job_done, n + 1)
                if kind == "q":
                    part_of = [t[:].rearrange("p (b g) q -> p b g q", g=NG)[:, c * B // 2:(c + 1) * B // 2, a, :] for t in (qh, ql)]
                    ins = nc.vector.tensor_tensor(part_of[1], bk[:, 0:HALF].rearrange("p (b q) -> p b q", q=TQ),
                                                  part_of[0].bitcast(F32), ALU.subtract)
                elif kind == "k":
                    lo, hi = kst[64:P, a * NG + 2 * c, 0:TK], kst[0:64, a * NG + 2 * c, 0:TK]
                    nc.vector.tensor_tensor(lo, bk[0:64, 0:TK], hi.bitcast(F32), ALU.subtract)
                    lo, hi = kst[0:64, a * NG + 2 * c + 1, 0:TK], kst[64:P, a * NG + 2 * c + 1, 0:TK]
                    ins = nc.vector.tensor_tensor(lo, bk[64:P, 0:TK], hi.bitcast(F32), ALU.subtract)
                else:
                    ins = nc.vector.tensor_copy(v_sb[:, a * NG:(a + 1) * NG, c, :, 0:DK],
                                                bk[0:KT, 0:DM].rearrange("p (g h d) -> p g h d", g=NG, h=GH))
                ins.then_inc(dve_evac, 1)

            def biased(j, m, i):
                if j % GH == 0:
                    dve.wait_ge(bias_ready, i + 1)
                if not (isinstance(m, int) and m < 4):
                    dve.wait_ge(t_ready, m - 3)
                made = m + 1 if isinstance(m, int) else dve.to_reg(m + 1)
                dve.wait_ge(pad_done, 1)
                dve.wait_ge(scores_ready, made)
                nc.vector.tensor_tensor_reduce(
                    out=prob[:, j % 4, 0:TK], in0=bank[j % 4][0:TQ, 0:TK], in1=mbias[:, (j // GH) % 2, j % GH, :],
                    scale=-1.0, scalar=3.0e38, op0=ALU.add, op1=ALU.min,
                    accum_out=nmax[:, j % 4:j % 4 + 1]).then_inc(z_done, 1)

            norm_steps = [0]

            def normalize(i, u):
                dve.wait_ge(o_ready, i * GH + GH)
                o = bank[6 + u][0:TQ, 0:GH * VW].rearrange("p (h w) -> p h w", w=VW)
                nc.vector.reciprocal(rden[:, u, :], o[:, :, DK]).then_inc(rden_done, 1)
                dve.wait_ge(rden_done, i + 1)
                nc.vector.tensor_tensor(
                    attn[:, bass.ds(i, 1), :].rearrange("p a (h d) -> p (a h) d", d=DK), o[:, :, 0:DK],
                    rden[:, u, :].unsqueeze(2).to_broadcast([TQ, GH, DK]), ALU.mult).then_inc(attn_done, 1)

            def two_steps(p, last):
                for j in range(8):
                    n = p * 8 + j
                    if not (last and j + 2 >= 8):
                        biased((j + 2) % 8, n + 2, p * 2 + (j + 2) // GH)
                    if j % 2 == 1:
                        dve.wait_ge(t_ready, n + 1)
                        if not (isinstance(n, int) and n < 4):
                            dve.wait_ge(o_ready, n - 3)
                        nc.vector.tensor_copy(pT[:, j % 4, :], bank[4 + j % 2][0:KT, 0:NT * TQ]).then_inc(pt_odd, 1)
                    if j == 1 and not (isinstance(p, int) and p == 0):
                        normalize(p * 2 - 1, 1)
                    if j == 5:
                        normalize(p * 2, 0)

            biased(0, 0, 0)
            biased(1, 1, 0)
            two_steps(0, False)
            with nc.vector.Fori(1, NI // 2 - 1) as p:
                two_steps(p, False)
            two_steps(NI // 2 - 1, True)
            normalize(NI - 1, 1)

            for r in range(9):
                dve.wait_ge(tail_act, r + 1)
                wcols = slice(r % 3 * 512, (r % 3 + 1) * 512)
                nc.vector.tensor_tensor(wT[:, r // 3, 1, wcols], bank[r % 8][:], wT[:, r // 3, 0, wcols].bitcast(F32),
                                        ALU.subtract).then_inc(tail_dve, 1)
            layer_norm(1)

            def scale_of(n, s_in):
                t, s, inv, f = (scl[:, n, c:c + 1] for c in range(4))
                dve.wait_ge(gmax_ready, n + 1)
                if s_in is None:
                    link(nc.vector.tensor_scalar(s, gmax[:, n:n + 1], 1.0 / ACT_QMAX, MIN_SCALE, ALU.mult, ALU.max))
                    nc.vector.reciprocal(inv, s).then_inc(scale_ready, 1)
                    return
                link(nc.vector.tensor_scalar(t, gmax[:, n:n + 1], s_in, 1.0 / ACT_QMAX, ALU.mult, ALU.mult))
                link(nc.vector.tensor_scalar(s, t, MIN_SCALE, None, ALU.max))
                link(nc.vector.reciprocal(inv, s))
                link(nc.vector.tensor_tensor(f, inv, s_in, ALU.mult))
                dve.sem_inc(scale_ready, 1)

            dve.wait_ge(xn_done, B)
            nc.vector.tensor_reduce(amax[0:TQ, 0:1], xn[:], AX.XY, ALU.max, apply_absolute_value=True).then_inc(amax_ready, 1)
            scale_of(0, None)
            dve.wait_ge(tail_act, A_GU)
            link(nc.vector.tensor_copy(xq[:, 0], x_int[:]))
            nc.vector.tensor_tensor(xq[:, 1], x_int[:], xq[:, 0].bitcast(F32), ALU.subtract).then_inc(tail_dve, 1)

            def maxima(n, m):
                for r in range(2 * FC):
                    dve.wait_ge(tail_act, A_GU + m * 2 * FC + r + 1)
                    ins = nc.vector.tensor_reduce(part[:, n, r:r + 1], (gate, up)[m][:, r // 2, r % 2 * HALF:(r % 2 + 1) * HALF],
                                                  AX.X, ALU.max, apply_absolute_value=True)
                link(ins)
                nc.vector.tensor_reduce(amax[:, n:n + 1], part[:, n, 0:2 * FC], AX.X, ALU.max).then_inc(amax_ready, 1)

            maxima(1, 0)
            scale_of(1, scl[:, 0, 1:2])
            for fc in range(FC):
                nc.vector.tensor_scalar(g_int[:, fc, :], gate[:, fc, :], scl[:, 1, 3:4], None, ALU.mult).then_inc(sint_ready, 1)
            maxima(2, 1)
            scale_of(2, scl[:, 0, 1:2])
            for fc in range(FC):
                nc.vector.tensor_scalar(u_int[:, fc, :], up[:, fc, :], scl[:, 2, 3:4], None, ALU.mult)
            for fc in range(FC):
                dve.wait_ge(sig_ready, fc + 1)
                link(nc.vector.tensor_scalar(s_int[:, fc, :], gate[:, fc, :], UBITS, None, ALU.mult))
                link(nc.vector.tensor_tensor(gate[:, fc, :], g_int[:, fc, :], s_int[:, fc, :], ALU.mult))
                ins = nc.vector.tensor_reduce(part[:, 3, fc:fc + 1], gate[:, fc, :], AX.X, ALU.max, apply_absolute_value=True)
            link(ins)
            nc.vector.tensor_reduce(amax[:, 3:4], part[:, 3, 0:FC], AX.X, ALU.max).then_inc(amax_ready, 1)
            unit = scl[:, 0, 3:4]
            link(nc.vector.tensor_scalar(unit, scl[:, 1, 1:2], 1.0 / UBITS, None, ALU.mult))
            scale_of(3, unit)
            for fc in range(FC):
                link(nc.vector.tensor_scalar(g_int[:, fc, :], gate[:, fc, :], scl[:, 3, 3:4], None, ALU.mult))
                link(nc.vector.tensor_tensor(up[:, fc, :], g_int[:, fc, :], u_int[:, fc, :], ALU.mult))
                ins = nc.vector.tensor_reduce(part[:, 4, fc:fc + 1], up[:, fc, :], AX.X, ALU.max, apply_absolute_value=True)
            link(ins)
            nc.vector.tensor_reduce(amax[:, 4:5], part[:, 4, 0:FC], AX.X, ALU.max).then_inc(amax_ready, 1)
            unit = scl[:, 0, 0:1]
            link(nc.vector.tensor_tensor(unit, scl[:, 3, 1:2], scl[:, 2, 1:2], ALU.mult))
            scale_of(4, unit)
            for fc in range(FC):
                link(nc.vector.tensor_scalar(g_int[:, fc, :], up[:, fc, :], scl[:, 4, 3:4], None, ALU.mult))
                link(nc.vector.tensor_copy(oq[0][:, fc, :], g_int[:, fc, :]))
                ins = nc.vector.tensor_tensor(oq[1][:, fc, :], g_int[:, fc, :], oq[0][:, fc, :].bitcast(F32), ALU.subtract)
            ins.then_inc(tail_dve, 1)
            for c in range(B // 2):
                dve.wait_ge(tail_pe, P_GU + c + 1)
                nc.vector.scalar_tensor_tensor(
                    out=x_sb[:, 2 * c:2 * c + 2, :].rearrange("p j d -> p (j d)"), in0=bank[c][0:TQ, :],
                    scalar=scl[0:TQ, 4, 1:2], in1=x_sb[:, 2 * c:2 * c + 2, :].rearrange("p j d -> p (j d)"),
                    op0=ALU.mult, op1=ALU.add).then_inc(tail_dve, 1)


def kernel(x, ctx_1024, mask_Bx1x1xS2_bk0, L0_xattn_Wq, L0_xattn_Wk, L0_xattn_Wv, L0_xattn_Wo, L0_xattn_rel_bias,
           L0_ffn_w_gate, L0_ffn_w_up, L0_ffn_w_down):
    import concourse.bacc as bacc
    from concourse.bass_utils import run_bass_kernel_spmd

    wq = np.asarray(L0_xattn_Wq).T.reshape(DM, NG, 1, GH * DK)
    onehot = np.zeros((NBUCKET, NREL), np.float32)
    for r in range(NREL):
        onehot[bucket_of(r - (TQ - 1)), r] = 1.0
    rows = np.arange(P) % (GH * DK) // DK
    layout = {
        "x": np.asarray(x)[:, ::-1],
        "ctxT": np.asarray(ctx_1024).reshape(B * TK, DM).T,
        "mask": np.asarray(mask_Bx1x1xS2_bk0).reshape(B, TK),
        "wqT": np.concatenate([wq, wq], axis=2).reshape(DM, NG, P),
        "wkT": np.asarray(L0_xattn_Wk).T,
        "wvT": np.asarray(L0_xattn_Wv).T,
        "woT": np.asarray(L0_xattn_Wo).T,
        "relT": np.asarray(L0_xattn_rel_bias).T,
        "w_gate": np.asarray(L0_ffn_w_gate),
        "w_up": np.asarray(L0_ffn_w_up),
        "w_down": np.asarray(L0_ffn_w_down),
        "onehot": onehot,
        "hmask": (rows[:, None] == np.arange(GH)[None, :]).astype(np.float32),
        "ident": np.eye(P, dtype=np.float32),
    }
    nc = bacc.Bacc("TRN2", target_bir_lowering=False, num_devices=1)
    arrays, args = {}, []
    for name, a in layout.items():
        a = np.ascontiguousarray(a)
        arrays[f"in_{name}"] = a
        args.append(nc.dram_tensor(f"in_{name}", a.shape, mybir.dt.from_np(a.dtype), kind="ExternalInput").ap())
    out = nc.dram_tensor("out_y", (B, TQ, DM), F32, kind="ExternalOutput").ap()
    build(nc, *args, out)
    r = run_bass_kernel_spmd(nc, [arrays], core_ids=[0])
    return np.ascontiguousarray(r.results[0]["out_y"][:, ::-1])
```

```python
from contextlib import ExitStack

import numpy as np

import concourse.bass as bass
from concourse import mybir

ALU = mybir.AluOpType
ACT = mybir.ActivationFunctionType
AX = mybir.AxisListType
F32 = mybir.dt.float32
F32R = mybir.dt.float32r
BF16 = mybir.dt.bfloat16
I16 = mybir.dt.int16
U16 = mybir.dt.uint16
U8 = mybir.dt.uint8
RMAX = bass.bass_isa.ReduceOp.max

P = 128
B, TQ, TK, DM = 8, 100, 361, 256
H, DK = 16, 16
GH = 4
NG = H // GH
NI = B * NG
NH = NI * GH
KC = DM // P
NT = 3
KT = (TK + NT - 1) // NT
TKE = TK + TK % 2
TKP = NT * KT
HW = 4 * DK
PW = 2 * (HW + DK)
NTOK = B * TQ
HALF = NTOK // 2
FF = 768
FC = FF // P
WBLK = 32
NBLK = FC * DM // WBLK
NREL = TQ + TK - 1
NBUCKET = 32
MASKED = float(2.0 ** 100)
LN_EPS = 1e-5
PRODUCTS = [(0, 0), (0, 1), (1, 0)]
ACT_QMAX = 32767.0
W_QMAX = 7.0
MIN_SCALE = 1e-12
UBITS = 65536.0
ROUND = 1.5 * 2.0 ** 23

FAR_FROM = [8, 12, 16, 23, 32, 46, 64, 91]


def bucket_of(rel):
    dist = abs(rel)
    bucket = dist if dist < 8 else 7 + sum(dist >= d for d in FAR_FROM)
    return bucket + (NBUCKET // 2 if rel > 0 else 0)


def build(nc, x, ctxT, mask, wqT, wkT, wvT, woT, relT, w_gate, w_up, w_down, onehot, hmask, ident, out):
    rel_row = nc.dram_tensor("rel_row", [H, NREL], F32, kind="Internal")

    with ExitStack() as ctx:
        def sb(name, shape, dt=F32):
            return ctx.enter_context(nc.sbuf_tensor(name, shape, dt))

        def sem(name):
            return ctx.enter_context(nc.semaphore(name))

        bank = [ctx.enter_context(nc.psum_tensor(f"bank{n}", [P, 512], F32)) for n in range(8)]

        region_ctx = sb("region_ctx", [P, B * KC * TKP])
        region_bias = sb("region_bias", [P, H * TK])
        region_v = sb("region_v", [P, NI * NT * GH * DK])
        region_ffw = sb("region_ffw", [P, 3 * FC * DM])
        region_w = sb("region_w", [P, 3 * KC * DM])
        region_q = sb("region_q", [P, 2 * NI * TQ], F32R)
        region_k = sb("region_k", [P, NI * TKE], F32R)
        region_x = sb("region_x", [P, B * DM])
        region_xT = sb("region_xT", [P, KC * NTOK])
        x_sb = sb("x_sb", [TQ, B, DM])
        wo_sb = sb("wo_sb", [P, KC, DM])
        rel_sb = sb("rel_sb", [NBUCKET, H])
        hmask_sb = sb("hmask_sb", [P, GH])
        ident_sb = sb("ident_sb", [P, P])

        ctxT_sb = region_ctx[:].rearrange("p (b c n) -> p b c n", b=B, c=KC)
        wq_sb = region_w[:, 0:2 * KC * DM].rearrange("p (c g m) -> p c g m", c=KC, g=NG)
        wk_sb = region_w[:, 2 * KC * DM:].rearrange("p (c m) -> p c m", c=KC)
        wv_sb = sb("wv_sb", [P, KC, DM])
        onehot_sb = region_bias[0:NBUCKET, 0:NREL]
        mask_u8 = region_v[0:TQ, 0:B * TK // 4].bitcast(U8)
        ffw = region_ffw[:].rearrange("p (m n) -> p m n", m=3)
        relrow_sb = region_bias[0:H, NREL:2 * NREL]
        bias_sb = region_bias[0:TQ, :].rearrange("p (h n) -> p h n", h=H)
        mask_add = sb("mask_add", [TQ, B, TK], BF16)
        xn = region_x[0:TQ, :].rearrange("p (b d) -> p b d", b=B)
        xT = region_xT[:].rearrange("p (c n) -> p c n", c=KC)
        qh, ql = (region_q[:, m * NI * TQ:(m + 1) * NI * TQ].rearrange("p (i n) -> p i n", i=NI) for m in range(2))
        kst = region_k[:].rearrange("p (i n) -> p i n", i=NI)
        v_sb = region_v[0:KT, :].rearrange("p (i t h d) -> p i t h d", i=NI, t=NT, h=GH)
        qm = sb("qm", [P, 2, 2, GH, TQ], F32R)
        v_st = region_x[0:KT, 0:NT * GH * PW].rearrange("p (u t a w) -> p u t a w", u=2, t=NT, a=GH // 2)
        mbias = region_ctx[0:TQ, 0:2 * GH * TK].rearrange("p (u h n) -> p u h n", u=2, h=GH)
        prob = region_ctx[0:TQ, 4 * KC * TKP:4 * KC * TKP + 4 * TKP].rearrange("p (s n) -> p s n", s=4)
        pT = region_w[0:KT, 0:4 * NT * TQ].rearrange("p (s n) -> p s n", s=4)
        nmax = sb("nmax", [TQ, 4])
        rsum = sb("rsum", [P, 2, TQ])
        attnT = region_xT[:].rearrange("p (s n) -> p s n", s=NI // 2)
        stats = sb("stats", [TQ, B, 6])
        mv = sb("mv", [TQ, B, 2])
        veps = sb("veps", [TQ, B])
        rstd = sb("rstd", [TQ, B])
        mhalf = sb("mhalf", [TQ, B])
        wmax = sb("wmax", [P, 3, NBLK])
        wscale = sb("wscale", [P, 3, NBLK])
        winv = sb("winv", [P, 3, NBLK])
        part = sb("part", [P, 5, 2 * FC])
        amax = sb("amax", [P, 5])
        gmax = sb("gmax", [P, 5])
        scl = sb("scl", [P, 5, 4])
        unit = sb("unit", [P, 2])
        wT = region_k[:, 0:6 * FC * DM].rearrange("p (m s n) -> p m s n", m=3, s=2)
        xq = region_q[:, 0:2 * KC * NTOK].rearrange("p (s k n) -> p s k n", s=2, k=KC)
        oq = [t[:, 0:FC * NTOK].rearrange("p (k n) -> p k n", k=FC) for t in (region_q, region_k)]
        gate, up = (t[:, 0:FC * NTOK].rearrange("p (c n) -> p c n", c=FC) for t in (region_ctx, region_bias))
        g_int, u_int = (region_v[:, m * FC * NTOK // 2:(m + 1) * FC * NTOK // 2].bitcast(I16).rearrange("p (c n) -> p c n", c=FC)
                        for m in range(2))
        s_int = region_ffw[:, 0:FC * NTOK // 2].bitcast(U16).rearrange("p (c n) -> p c n", c=FC)
        x_int = region_w[:, 0:KC * NTOK // 2].bitcast(I16).rearrange("p (c n) -> p c n", c=KC)

        loaded = {n: sem(f"loaded_{n}") for n in ("x", "wq", "wk", "wv", "wo", "const", "mask", "ffw")}
        ctx_loaded = [sem(f"ctx_loaded{b}") for b in range(B)]
        relrow_stored, bias_loaded, out_stored = sem("relrow_stored"), sem("bias_loaded"), sem("out_stored")
        dve_step, pool_step = sem("dve_step"), sem("pool_step")
        ln_var, ln_rstd, xn_done = sem("ln_var"), sem("ln_rstd"), sem("xn_done")
        winv_done, wdiv_done, wround_done, ffw_done = sem("winv_done"), sem("wdiv_done"), sem("wround_done"), sem("ffw_done")
        fill_done, mask_done = sem("fill_done"), sem("mask_done")
        pad_done = sem("pad_done")
        job_done, act_evac, dve_evac = sem("job_done"), sem("act_evac"), sem("dve_evac")
        qm_high, qm_low, bias_ready, v_ready = sem("qm_high"), sem("qm_low"), sem("bias_ready"), sem("v_ready")
        scores_ready, z_done, prob_ready, t_ready = sem("scores_ready"), sem("z_done"), sem("prob_ready"), sem("t_ready")
        pt_ready = sem("pt_ready")
        o_ready, rsum_done, attn_done = sem("o_ready"), sem("rsum_done"), sem("attn_done")
        wo_made, res_done = sem("wo_made"), sem("res_done")
        w_turned, w_high, w_low = sem("w_turned"), sem("w_high"), sem("w_low")
        x_turned, xint_act, xint_dve = sem("x_turned"), sem("xint_act"), sem("xint_dve")
        x_high, x_low = sem("x_high"), sem("x_low")
        amax_ready, gmax_ready, scale_ready = sem("amax_ready"), sem("gmax_ready"), sem("scale_ready")
        gu_made, gu_copied, gint_done = sem("gu_made"), sem("gu_copied"), sem("gint_done")
        sig_done, sint_done, h_done = sem("sig_done"), sem("sint_done"), sem("h_done")
        uint_done, hint_done, o_done = sem("uint_done"), sem("hint_done"), sem("o_done")
        oint_done, o_high, o_low = sem("oint_done"), sem("o_high"), sem("o_low")
        down_made, y_done = sem("down_made"), sem("y_done")

        XT_BEFORE, Q_BEFORE = 3, 4
        def of_batch(b):
            return [("k", b, m) for m in range(KC)] + [("v", b, t) for t in range(NT)]

        jobs = [("rel", 0, 0)]
        for b in range(B):
            if b == XT_BEFORE:
                jobs += [("xT", c, 0) for c in range(B // 2)]
            if b == Q_BEFORE:
                jobs += [("q", g, hf) for hf in range(2) for g in range(NG)]
            jobs += of_batch(b)

        def on_dve(n):
            return jobs[n][0] in ("q", "k")

        def dve_after(n):
            return sum(on_dve(m) for m in range(n + 1))

        def bank_free(eng, n):
            if n >= 8:
                eng.wait_ge(act_evac, n - 7)
                if on_dve(n - 8):
                    eng.wait_ge(dve_evac, dve_after(n - 8))

        first_job, last_job = {}, {}
        for n, (kind, _, _) in enumerate(jobs):
            first_job.setdefault(kind, n)
            last_job[kind] = n
        half_used = jobs.index(("v", 3, NT - 1)) + 1

        WGROUPS = 9
        W_GATE, W_UP = 3, 6
        GROUPS = 4 * FC

        def group(r):
            return r // (2 * FC), r // FC % 2, r % FC

        FILLS = 7
        SCALES_AFTER, ROUND_AFTER = (2, 3, 4), (4, 5, 6)

        block = ctx.enter_context(nc.Block())

        @block.sync
        def _(sp):
            sp.dma_start(onehot_sb[:], onehot).then_inc(loaded["const"], 16)
            sp.dma_start(rel_sb[:], relT).then_inc(loaded["const"], 16)
            sp.dma_start(wk_sb, wkT.rearrange("(c p) m -> p c m", p=P)).then_inc(loaded["wk"], 16)
            for b in range(B):
                sp.dma_start(ctxT_sb[:, b], ctxT[:, b]).then_inc(ctx_loaded[b], 16)
            sp.wait_ge(act_evac, first_job["rel"] + 1)
            sp.dma_start(rel_row.ap(), relrow_sb[:]).then_inc(relrow_stored, 16)
            sp.wait_ge(relrow_stored, 16)
            window = bass.AP(rel_row, 0, [[1, TQ], [NREL, H], [1, TK]])
            sp.dma_start(bias_sb[:], window).then_inc(bias_loaded, 16)
            for c in range(B // 2):
                sp.wait_ge(y_done, 2 * c + 2)
                sp.dma_start(out[:, 2 * c:2 * c + 2, :], x_sb[:, 2 * c:2 * c + 2, :]).then_inc(out_stored, 16)
            sp.wait_ge(out_stored, 16 * (B // 2))

        def turned(c):
            return bank[c][:, 0:4 * TQ].rearrange("p (k n) -> p k n", k=KC)

        def of_tokens(t, c):
            return t[:, :, 2 * c * TQ:2 * (c + 1) * TQ]

        @block.gpsimd
        def _(pool):
            steps = [0]

            def link(ins):
                steps[0] += 1
                ins.then_inc(pool_step, 1)
                pool.wait_ge(pool_step, steps[0])

            pool.dma_start(mask_u8, mask.rearrange("b n -> (b n)").partition_broadcast(TQ)).then_inc(loaded["mask"], 16)
            nc.gpsimd.memset(mhalf[:], -0.5).then_inc(fill_done, 1)
            nc.gpsimd.memset(kst[:, :, TK:].bitcast(F32), 0.0).then_inc(fill_done, 1)
            nc.gpsimd.memset(amax[:], 0.0).then_inc(fill_done, 1)
            def rsqrt_of_var(n):
                pool.wait_ge(ln_var, n)
                link(nc.gpsimd.tensor_scalar(veps[:], mv[:, :, 1], LN_EPS, None, ALU.add))
                nc.gpsimd.tensor_tensor(rstd[:], veps[:], mhalf[:], ALU.pow).then_inc(ln_rstd, 1)

            rsqrt_of_var(1)

            pool.wait_ge(loaded["mask"], 16)
            nc.gpsimd.tensor_scalar(mask_add[:].rearrange("p b n -> p (b n)"), mask_u8, -1.0, MASKED,
                                    ALU.add, ALU.mult).then_inc(mask_done, 1)

            def prepare(b, g, i):
                u = g % 2
                pool.wait_ge(loaded["const"], 64)
                if not (isinstance(i, int) and i < 2):
                    pool.wait_ge(scores_ready, i * GH - GH)
                nc.gpsimd.tensor_tensor(
                    qm[:, u, 0], qh[:, bass.ds(i, 1), :].bitcast(F32).to_broadcast([P, GH, TQ]),
                    hmask_sb[:].unsqueeze(2).to_broadcast([P, GH, TQ]), ALU.mult).then_inc(qm_high, 1)
                pool.wait_ge(mask_done, 1)
                if not (isinstance(i, int) and i < 2):
                    pool.wait_ge(z_done, i * GH - GH)
                nc.gpsimd.tensor_tensor(
                    mbias[:, u], bias_sb[:, g * GH:(g + 1) * GH, :],
                    mask_add[:, bass.ds(b, 1), :].to_broadcast([TQ, GH, TK]), ALU.add).then_inc(bias_ready, 1)

            def blocks(m):
                return ffw[:, m, :].rearrange("p (n k) -> p n k", k=WBLK)

            for m in range(3):
                pool.wait_ge(winv_done, m + 1)
                nc.gpsimd.tensor_tensor(blocks(m), blocks(m), winv[:, m, :].unsqueeze(2).to_broadcast([P, NBLK, WBLK]),
                                        ALU.mult).then_inc(wdiv_done, 1)
            for m in range(3):
                pool.wait_ge(wround_done, m + 1)
                nc.gpsimd.tensor_tensor(blocks(m), blocks(m), wscale[:, m, :].unsqueeze(2).to_broadcast([P, NBLK, WBLK]),
                                        ALU.mult).then_inc(ffw_done, 1)

            pool.wait_ge(job_done, last_job["xT"] + 1)
            pairs = v_st[:].rearrange("p u t a w -> p (u t a) w")
            for at, n, value in ((0, 2 * DK, 0.0), (2 * DK, DK, 1.0), (3 * DK, HW, 0.0), (HW + 3 * DK, DK, 1.0)):
                nc.gpsimd.memset(pairs[:, :, at:at + n], value).then_inc(fill_done, 1)
            pool.wait_ge(act_evac, last_job["q"] + 1)
            pool.wait_ge(dve_evac, dve_after(last_job["q"]))
            pool.wait_ge(bias_loaded, 16)
            pool.wait_ge(job_done, half_used)
            for g in range(NG):
                prepare(0, g, g)
            with nc.gpsimd.Fori(1, B) as b:
                for g in range(NG):
                    prepare(b, g, b * NG + g)

            rsqrt_of_var(2)

            def over_partitions(n):
                pool.wait_ge(amax_ready, n + 1)
                nc.gpsimd.partition_all_reduce(gmax[:, n:n + 1], amax[:, n:n + 1], P, RMAX).then_inc(gmax_ready, 1)

            for n in range(5):
                over_partitions(n)

        @block.tensor
        def _(pe):
            pe.wait_ge(loaded["const"], 64)
            for n, (kind, a, c) in enumerate(jobs):
                bk = bank[n % 8]
                bank_free(pe, n)
                if kind == "rel":
                    mm = nc.tensor.matmul(bk[0:H, 0:NREL], rel_sb[:], onehot_sb[:], start=True, stop=True)
                elif kind == "xT":
                    pe.wait_ge(xn_done, a + 1)
                    for j in range(2):
                        for k in range(KC):
                            mm = nc.tensor.transpose(bk[:, (2 * k + j) * TQ:(2 * k + j + 1) * TQ],
                                                     xn[:, 2 * a + j, k * P:(k + 1) * P], ident_sb[0:TQ, 0:TQ])
                elif kind == "q":
                    if n == first_job["q"]:
                        pe.wait_ge(loaded["wq"], 16)
                        pe.wait_ge(act_evac, last_job["xT"] + 1)
                    for k in range(KC):
                        mm = nc.tensor.matmul(bk[:, 0:HALF], wq_sb[:, k, a, :], xT[:, k, c * HALF:(c + 1) * HALF],
                                              start=(k == 0), stop=(k == KC - 1))
                elif kind == "k":
                    if n == first_job["k"]:
                        pe.wait_ge(loaded["wk"], 16)
                    if c == 0:
                        pe.wait_ge(ctx_loaded[a], 16)
                    for k in range(KC):
                        mm = nc.tensor.matmul(bk[:, 0:TK], wk_sb[:, k, c * P:(c + 1) * P],
                                              ctxT_sb[:, a, k, 0:TK], start=(k == 0), stop=(k == KC - 1))
                elif kind == "v":
                    if n == first_job["v"]:
                        pe.wait_ge(loaded["wv"], 16)
                    for k in range(KC):
                        mm = nc.tensor.matmul(bk[0:KT, 0:DM], ctxT_sb[:, a, k, c * KT:(c + 1) * KT], wv_sb[:, k, :],
                                              start=(k == 0), stop=(k == KC - 1))
                mm.then_inc(job_done, 1)

            pe.wait_ge(act_evac, len(jobs))
            pe.wait_ge(dve_evac, dve_after(len(jobs) - 1))

            def scores(step2, j, m, i, first):
                bk = bank[j % 4]
                u = (j // GH) % 2
                if j % GH == 0:
                    pe.wait_ge(qm_high, i + 1)
                    pe.wait_ge(qm_low, i + 1)
                if not first:
                    pe.wait_ge(z_done, m - 3)
                for part_no in range(2):
                    mm = nc.tensor.matmul(bk[0:TQ, 0:TKE], qm[:, u, part_no, j % GH, :],
                                          kst[:, bass.ds(i, 1), :].rearrange("p a n -> p (a n)"),
                                          start=(part_no == 0), stop=(part_no == 1))
                mm.then_inc(scores_ready, 1)

            def weigh(p, j):
                i = p * 2 + j // GH
                u, pair, second = j // GH, j % GH // 2, j % 2
                o = bank[6 + u][pair * HW:(pair + 1) * HW, 0:TQ]
                pe.wait_ge(pt_ready, p * 8 + j + 1)
                if j % GH == 0:
                    pe.wait_ge(v_ready, i + 1)
                    if not (isinstance(i, int) and i < 2):
                        pe.wait_ge(attn_done, i - 1)
                for t in range(NT):
                    mm = nc.tensor.matmul(o, v_st[:, u, t, pair, second * HW:(second + 1) * HW],
                                          pT[:, j % 4, t * TQ:(t + 1) * TQ],
                                          start=(not second and t == 0), stop=(bool(second) and t == NT - 1))
                mm.then_inc(o_ready, 1)

            def two_steps(p, last):
                static = isinstance(p, int)
                for j in range(8):
                    if not (last and j + 3 >= 8):
                        m = p * 8 + (j + 3)
                        jj = (j + 3) % 8
                        scores(None, jj, m, p * 2 + (j + 3) // GH, static and m < 4)
                    n = p * 8 + j
                    bk = bank[4 + j % 2]
                    pe.wait_ge(prob_ready, n + 1)
                    if not (static and n < 2):
                        pe.wait_ge(pt_ready, n - 1)
                    for t in range(NT):
                        mm = nc.tensor.transpose(bk[0:KT, t * TQ:(t + 1) * TQ], prob[:, j % 4, t * KT:(t + 1) * KT],
                                                 ident_sb[0:TQ, 0:TQ])
                    mm.then_inc(t_ready, 1)
                    if j > 0:
                        weigh(p, j - 1)
                    elif not (static and p == 0):
                        weigh(p - 1, 7)

            pe.wait_ge(fill_done, FILLS)
            pe.wait_ge(pad_done, 1)
            for m in range(3):
                scores(None, m, m, 0, True)
            two_steps(0, False)
            with nc.tensor.Fori(1, NI // 2 - 1) as p:
                two_steps(p, False)
            two_steps(NI // 2 - 1, True)
            weigh(NI // 2 - 1, 7)

            def turn_weights(r):
                m, c = r // 3, r % 3
                bk = bank[4 + r % 4]
                if r >= 4:
                    pe.wait_ge(w_low, r - 3)
                for j in range(4):
                    n = 4 * c + j
                    at = (n % FC) * DM + (n // FC) * P if m < 2 else (n % KC) * FF + (n // KC) * P
                    mm = nc.tensor.transpose(bk[:, j * P:(j + 1) * P], ffw[:, m, at:at + P], ident_sb[:])
                mm.then_inc(w_turned, 1)

            pe.wait_ge(ffw_done, 3)
            pe.wait_ge(pt_ready, NH)
            pe.wait_ge(z_done, NH)
            turn_weights(0)
            turn_weights(1)
            pe.wait_ge(loaded["wo"], 16)
            for c in range(B // 2):
                pe.wait_ge(attn_done, 2 * NG * (c + 1))
                for j in range(2):
                    for k in range(KC):
                        mm = nc.tensor.matmul(bank[c][0:TQ, j * DM:(j + 1) * DM], attnT[:, (2 * c + j) * KC + k, :],
                                              wo_sb[:, k, :], start=(k == 0), stop=(k == KC - 1))
                mm.then_inc(wo_made, 1)
            for r in range(2, 6):
                turn_weights(r)
            for c in range(B // 2):
                pe.wait_ge(res_done, c + 1)
                pe.wait_ge(xn_done, B // 2 + c + 1)
                for j in range(2):
                    for k in range(KC):
                        mm = nc.tensor.transpose(bank[c][:, (2 * k + j) * TQ:(2 * k + j + 1) * TQ],
                                                 xn[:, 2 * c + j, k * P:(k + 1) * P], ident_sb[0:TQ, 0:TQ])
                mm.then_inc(x_turned, 1)
            for r in range(6, WGROUPS):
                turn_weights(r)
            pe.wait_ge(w_low, W_GATE)
            for r in range(GROUPS):
                m, hf, fc = group(r)
                if fc == 0 and m == 0:
                    pe.wait_ge(x_low, B // 4 * (hf + 1))
                if r == 4:
                    pe.wait_ge(w_low, WGROUPS)
                if r >= 8:
                    pe.wait_ge(gu_copied, r - 7)
                for k in range(KC):
                    for ws, xs in PRODUCTS:
                        mm = nc.tensor.matmul(bank[r % 8][:, 0:HALF], wT[:, m, ws, k * FF + fc * P:k * FF + (fc + 1) * P],
                                              xq[:, xs, k, hf * HALF:(hf + 1) * HALF], start=(k == 0 and (ws, xs) == PRODUCTS[0]),
                                              stop=(k == KC - 1 and (ws, xs) == PRODUCTS[-1]))
                mm.then_inc(gu_made, 1)

            def down(b, k, ws, xs):
                first, final = (k == 0 and (ws, xs) == PRODUCTS[0]), (k == FC - 1 and (ws, xs) == (0, 1))
                return nc.tensor.matmul(bank[b][0:TQ, 0:DM], oq[xs][:, k, b * TQ:(b + 1) * TQ],
                                        wT[:, 2, ws, k * DM:(k + 1) * DM], start=first, stop=final)

            pe.wait_ge(gu_copied, GROUPS)
            for k in range(FC - 1):
                pe.wait_ge(o_high, k + 1)
                for b in range(B):
                    down(b, k, 0, 0)
                    down(b, k, 1, 0)
                pe.wait_ge(o_low, k + 1)
                for b in range(B):
                    down(b, k, 0, 1)
            pe.wait_ge(o_low, FC)
            for b in range(B):
                down(b, FC - 1, 0, 0)
                down(b, FC - 1, 1, 0)
                down(b, FC - 1, 0, 1).then_inc(down_made, 1)

        @block.scalar
        def _(act):
            act.dma_start(x_sb[:], x).then_inc(loaded["x"], 16)
            act.dma_start(ident_sb[:], ident).then_inc(loaded["const"], 16)
            act.dma_start(hmask_sb[:], hmask).then_inc(loaded["const"], 16)
            act.dma_start(wv_sb[:], wvT.rearrange("(c p) m -> p c m", p=P)).then_inc(loaded["wv"], 16)
            act.dma_start(wq_sb, wqT.rearrange("(c p) g m -> p c g m", p=P)).then_inc(loaded["wq"], 16)
            act.dma_start(ffw[:, 0, :].rearrange("p (c i) -> p c i", c=FC),
                          w_gate.rearrange("(c p) i -> p c i", p=P)).then_inc(loaded["ffw"], 16)
            act.dma_start(ffw[:, 1, :].rearrange("p (c i) -> p c i", c=FC),
                          w_up.rearrange("(c p) i -> p c i", p=P)).then_inc(loaded["ffw"], 16)
            act.dma_start(ffw[:, 2, :].rearrange("p (c i) -> p c i", c=KC),
                          w_down.rearrange("(c p) i -> p c i", p=P)).then_inc(loaded["ffw"], 16)
            act.dma_start(wo_sb[:], woT.rearrange("(c p) m -> p c m", p=P)).then_inc(loaded["wo"], 16)

            for n, (kind, a, c) in enumerate(jobs):
                bk = bank[n % 8]
                act.wait_ge(job_done, n + 1)
                if kind == "rel":
                    ins = nc.scalar.copy(relrow_sb[:], bk[0:H, 0:NREL])
                elif kind == "xT":
                    ins = nc.scalar.copy(xT[:, :, 2 * a * TQ:2 * (a + 1) * TQ],
                                         bk[:, 0:4 * TQ].rearrange("p (k n) -> p k n", k=KC))
                elif kind == "q":
                    ins = nc.scalar.copy(
                        qh[:].rearrange("p (b g) q -> p b g q", g=NG)[:, c * B // 2:(c + 1) * B // 2, a, :],
                        bk[:, 0:HALF].rearrange("p (b q) -> p b q", q=TQ))
                elif kind == "k":
                    nc.scalar.copy(kst[0:64, a * NG + 2 * c, 0:TK], bk[0:64, 0:TK])
                    ins = nc.scalar.copy(kst[64:P, a * NG + 2 * c + 1, 0:TK], bk[64:P, 0:TK])
                else:
                    if n == first_job["v"]:
                        act.wait_ge(mask_done, 1)
                    ins = nc.scalar.copy(v_sb[:, a * NG:(a + 1) * NG, c],
                                         bk[0:KT, 0:DM].rearrange("p (g h d) -> p g h d", g=NG, h=GH))
                ins.then_inc(act_evac, 1)

            def stage_values(i, u):
                if not (isinstance(i, int) and i < 2):
                    act.wait_ge(o_ready, i * GH - GH)
                nc.scalar.copy(v_st[:, u].rearrange("p t a (c w) -> p (t a) c w", c=2)[:, :, :, 0:DK],
                               v_sb[:, bass.ds(i, 1)].rearrange("p i t (a c) d -> p (i t a) c d", c=2)).then_inc(v_ready, 1)

            def exponent(p, j, m):
                act.wait_ge(z_done, m + 1)
                nc.scalar.activation(prob[:, j % 4, 0:TK], prob[:, j % 4, 0:TK], ACT.Exp, bias=nmax[:, j % 4:j % 4 + 1],
                                     scale=-1.0).then_inc(prob_ready, 1)

            def two_steps(p, last):
                for j in range(8):
                    n = p * 8 + j
                    if not (last and j == 7):
                        exponent(p, (j + 1) % 8, n + 1)
                    act.wait_ge(t_ready, n + 1)
                    if not (isinstance(n, int) and n < 4):
                        act.wait_ge(o_ready, n - 3)
                    nc.scalar.copy(pT[:, j % 4, :], bank[4 + j % 2][0:KT, 0:NT * TQ]).then_inc(pt_ready, 1)
                    if j == 1:
                        stage_values(p * 2 + 1, 1)
                    if j == 5 and not last:
                        stage_values(p * 2 + 2, 0)

            act.wait_ge(fill_done, FILLS)
            act.wait_ge(act_evac, len(jobs))
            stage_values(0, 0)
            exponent(0, 0, 0)
            two_steps(0, False)
            with nc.scalar.Fori(1, NI // 2 - 1) as p:
                two_steps(p, False)
            two_steps(NI // 2 - 1, True)

            def weights_high(r):
                act.wait_ge(w_turned, r + 1)
                nc.scalar.copy(wT[:, r // 3, 0, r % 3 * 512:(r % 3 + 1) * 512], bank[4 + r % 4][:]).then_inc(w_high, 1)

            for r in range(6):
                weights_high(r)
            act.wait_ge(scale_ready, 1)
            for c in range(B // 4):
                act.wait_ge(x_turned, c + 1)
                nc.scalar.activation(of_tokens(x_int, c), turned(c), ACT.Copy, scale=scl[:, 0, 2:3]).then_inc(xint_act, 1)
            for c in range(B // 2):
                if c < B // 4:
                    act.wait_ge(xint_act, c + 1)
                else:
                    act.wait_ge(xint_dve, c - B // 4 + 1)
                nc.scalar.copy(of_tokens(xq[:, 0], c), of_tokens(x_int, c)).then_inc(x_high, 1)
            for r in range(6, WGROUPS):
                weights_high(r)

            def copy_group(r):
                m, hf, fc = group(r)
                act.wait_ge(gu_made, r + 1)
                nc.scalar.copy((gate, up)[m][:, fc, hf * HALF:(hf + 1) * HALF], bank[r % 8][:, 0:HALF]).then_inc(gu_copied, 1)

            for r in range(2 * FC + 2):
                copy_group(r)
            act.wait_ge(scale_ready, 2)
            for fc in range(FC):
                act.wait_ge(gint_done, fc + 1)
                nc.scalar.activation(gate[:, fc, :], g_int[:, fc, :], ACT.Sigmoid, scale=scl[:, 1, 1:2]).then_inc(sig_done, 1)
                if fc < FC - 1:
                    copy_group(2 * FC + 2 + 2 * fc)
                act.wait_ge(sig_done, fc + 1)
                nc.scalar.activation(s_int[:, fc, :], gate[:, fc, :], ACT.Copy, scale=UBITS).then_inc(sint_done, 1)
                if fc < FC - 1:
                    copy_group(2 * FC + 3 + 2 * fc)
            act.wait_ge(scale_ready, 3)
            for fc in range(FC):
                nc.scalar.activation(u_int[:, fc, :], up[:, fc, :], ACT.Copy, scale=scl[:, 2, 3:4]).then_inc(uint_done, 1)
                if fc > 0:
                    act.wait_ge(scale_ready, 4)
                    nc.scalar.activation(g_int[:, fc, :], gate[:, fc, :], ACT.Copy, scale=scl[:, 3, 3:4]).then_inc(hint_done, 1)

        @block.vector
        def _(dve):
            steps = [0]

            def link(ins):
                steps[0] += 1
                ins.then_inc(dve_step, 1)
                dve.wait_ge(dve_step, steps[0])

            def variance():
                for b in range(B):
                    ins = nc.vector.bn_aggr(mv[:, b, :], stats[:, b, :])
                ins.then_inc(ln_var, 1)

            def normalize_tokens(b):
                ins = nc.vector.tensor_scalar(xn[:, b, :], x_sb[:, b, :], mv[:, b, 0:1], rstd[:, b:b + 1],
                                              ALU.subtract, ALU.mult)
                if b % 2 == 1:
                    ins.then_inc(xn_done, 1)

            def weight_scales(m):
                link(nc.vector.tensor_reduce(wmax[:, m, :], ffw[:, m, :].rearrange("p (n k) -> p n k", k=WBLK), AX.X, ALU.max,
                                             apply_absolute_value=True))
                link(nc.vector.tensor_scalar(wscale[:, m, :], wmax[:, m, :], 1.0 / W_QMAX, MIN_SCALE, ALU.mult, ALU.max))
                nc.vector.reciprocal(winv[:, m, :], wscale[:, m, :]).then_inc(winv_done, 1)

            def round_weights(m):
                dve.wait_ge(wdiv_done, m + 1)
                link(nc.vector.tensor_scalar(ffw[:, m, :], ffw[:, m, :], ROUND, -ROUND, ALU.add, ALU.add))
                nc.vector.tensor_scalar(ffw[:, m, :], ffw[:, m, :], W_QMAX, -W_QMAX - 1.0, ALU.min, ALU.max).then_inc(wround_done, 1)

            dve.wait_ge(loaded["x"], 16)
            for b in range(B):
                ins = nc.vector.bn_stats(stats[:, b, :], x_sb[:, b, :])
            link(ins)
            variance()
            for n, (kind, a, c) in enumerate(jobs):
                if not on_dve(n):
                    continue
                bk = bank[n % 8]
                dve.wait_ge(act_evac, n + 1)
                if kind == "q":
                    part_of = [t[:].rearrange("p (b g) q -> p b g q", g=NG)[:, c * B // 2:(c + 1) * B // 2, a, :] for t in (qh, ql)]
                    ins = nc.vector.tensor_tensor(part_of[1], bk[:, 0:HALF].rearrange("p (b q) -> p b q", q=TQ),
                                                  part_of[0].bitcast(F32), ALU.subtract)
                else:
                    lo, hi = kst[64:P, a * NG + 2 * c, 0:TK], kst[0:64, a * NG + 2 * c, 0:TK]
                    nc.vector.tensor_tensor(lo, bk[0:64, 0:TK], hi.bitcast(F32), ALU.subtract)
                    lo, hi = kst[0:64, a * NG + 2 * c + 1, 0:TK], kst[64:P, a * NG + 2 * c + 1, 0:TK]
                    ins = nc.vector.tensor_tensor(lo, bk[64:P, 0:TK], hi.bitcast(F32), ALU.subtract)
                ins.then_inc(dve_evac, 1)
                if (kind, c) == ("k", KC - 1):
                    if a == 0:
                        dve.wait_ge(ln_rstd, 1)
                        for b in range(B):
                            normalize_tokens(b)
                    if a in SCALES_AFTER:
                        dve.wait_ge(loaded["ffw"], 48)
                        weight_scales(SCALES_AFTER.index(a))
                    if a in ROUND_AFTER:
                        round_weights(ROUND_AFTER.index(a))

            def mask_low(i, u):
                if not (isinstance(i, int) and i < 2):
                    dve.wait_ge(scores_ready, i * GH - GH)
                for h in range(GH):
                    ins = nc.vector.tensor_scalar(qm[:, u, 1, h, :], ql[:, bass.ds(i, 1), :].rearrange("p a n -> p (a n)").bitcast(F32),
                                                  hmask_sb[:, h:h + 1], None, ALU.mult)
                ins.then_inc(qm_low, 1)

            def biased(j, m, i):
                if j % GH == 0:
                    dve.wait_ge(bias_ready, i + 1)
                if not (isinstance(m, int) and m < 4):
                    dve.wait_ge(t_ready, m - 3)
                made = m + 1 if isinstance(m, int) else dve.to_reg(m + 1)
                dve.wait_ge(pad_done, 1)
                dve.wait_ge(scores_ready, made)
                nc.vector.tensor_tensor_reduce(
                    out=prob[:, j % 4, 0:TK], in0=bank[j % 4][0:TQ, 0:TK], in1=mbias[:, (j // GH) % 2, j % GH, :],
                    scale=-1.0, scalar=3.0e38, op0=ALU.add, op1=ALU.min,
                    accum_out=nmax[:, j % 4:j % 4 + 1]).then_inc(z_done, 1)

            def normalize(i, u, s):
                dve.wait_ge(o_ready, i * GH + GH)
                o = bank[6 + u]
                nc.vector.reciprocal(rsum[:, u, :], o[:, 0:TQ]).then_inc(rsum_done, 1)
                dve.wait_ge(rsum_done, i + 1)
                for pair in range(2):
                    values, sums = pair * HW, pair * HW + 2 * DK
                    rows = (2 * u + pair) * 2 * DK
                    ins = nc.vector.tensor_tensor(
                        attnT[rows:rows + 2 * DK, bass.ds(s, 1), :].rearrange("p a n -> p (a n)"), o[values:values + 2 * DK, 0:TQ],
                        rsum[sums:sums + 2 * DK, u, :], ALU.mult)
                ins.then_inc(attn_done, 1)

            def two_steps(p, last):
                for j in range(8):
                    if not (last and j + 2 >= 8):
                        biased((j + 2) % 8, p * 8 + j + 2, p * 2 + (j + 2) // GH)
                    if j == 1 and not (isinstance(p, int) and p == 0):
                        normalize(p * 2 - 1, 1, p - 1)
                    if j == 5:
                        normalize(p * 2, 0, p)
                    if j % GH == 2 and not last:
                        mask_low(p * 2 + 2 + j // GH, j // GH)

            dve.wait_ge(job_done, len(jobs))
            nc.vector.memset(prob[:, :, TK:], 0.0).then_inc(pad_done, 1)
            dve.wait_ge(dve_evac, dve_after(len(jobs) - 1))
            mask_low(0, 0)
            mask_low(1, 1)
            biased(0, 0, 0)
            biased(1, 1, 0)
            two_steps(0, False)
            with nc.vector.Fori(1, NI // 2 - 1) as p:
                two_steps(p, False)
            two_steps(NI // 2 - 1, True)
            normalize(NI - 1, 1, NI // 2 - 1)

            def weights_low(r):
                dve.wait_ge(w_high, r + 1)
                wcols = slice(r % 3 * 512, (r % 3 + 1) * 512)
                nc.vector.tensor_tensor(wT[:, r // 3, 1, wcols], bank[4 + r % 4][:], wT[:, r // 3, 0, wcols].bitcast(F32),
                                        ALU.subtract).then_inc(w_low, 1)

            weights_low(0)
            weights_low(1)
            for c in range(B // 2):
                dve.wait_ge(wo_made, c + 1)
                pair = x_sb[:, 2 * c:2 * c + 2, :]
                nc.vector.tensor_tensor(pair, bank[c][0:TQ, :].rearrange("p (j d) -> p j d", j=2), pair,
                                        ALU.add).then_inc(res_done, 1)
                dve.wait_ge(res_done, c + 1)
                for b in (2 * c, 2 * c + 1):
                    ins = nc.vector.bn_stats(stats[:, b, :], x_sb[:, b, :])
            link(ins)
            variance()
            weights_low(2)
            weights_low(3)
            dve.wait_ge(ln_rstd, 2)
            for c in range(B // 2 + 1):
                if c < B // 2:
                    normalize_tokens(2 * c)
                    normalize_tokens(2 * c + 1)
                if c > 0:
                    dve.wait_ge(xn_done, B // 2 + c)
                    ins = nc.vector.tensor_reduce(part[0:TQ, 0, c - 1:c], xn[:, 2 * c - 2:2 * c, :], AX.XY, ALU.max,
                                                  apply_absolute_value=True)
            link(ins)
            nc.vector.tensor_reduce(amax[0:TQ, 0:1], part[0:TQ, 0, 0:B // 2], AX.X, ALU.max).then_inc(amax_ready, 1)
            weights_low(4)

            def scale_of(n, s_in):
                t, s, inv, f = (scl[:, n, c:c + 1] for c in range(4))
                dve.wait_ge(gmax_ready, n + 1)
                if s_in is None:
                    link(nc.vector.tensor_scalar(s, gmax[:, n:n + 1], 1.0 / ACT_QMAX, MIN_SCALE, ALU.mult, ALU.max))
                    nc.vector.reciprocal(inv, s).then_inc(scale_ready, 1)
                    return
                link(nc.vector.tensor_scalar(t, gmax[:, n:n + 1], s_in, 1.0 / ACT_QMAX, ALU.mult, ALU.mult))
                link(nc.vector.tensor_scalar(s, t, MIN_SCALE, None, ALU.max))
                link(nc.vector.reciprocal(inv, s))
                link(nc.vector.tensor_tensor(f, inv, s_in, ALU.mult))
                dve.sem_inc(scale_ready, 1)

            scale_of(0, None)
            dve.wait_ge(scale_ready, 1)
            for c in range(B // 4, B // 2):
                dve.wait_ge(x_turned, c + 1)
                nc.vector.tensor_scalar(of_tokens(x_int, c), turned(c), scl[:, 0, 2:3], None, ALU.mult).then_inc(xint_dve, 1)
            for c in range(B // 2):
                dve.wait_ge(x_high, c + 1)
                nc.vector.tensor_tensor(of_tokens(xq[:, 1], c), of_tokens(x_int, c), of_tokens(xq[:, 0], c).bitcast(F32),
                                        ALU.subtract).then_inc(x_low, 1)
            for r in range(5, WGROUPS):
                weights_low(r)

            def largest_of_group(r):
                m, hf, fc = group(r)
                dve.wait_ge(gu_copied, r + 1)
                return nc.vector.tensor_reduce(part[:, 1 + m, hf * FC + fc:hf * FC + fc + 1],
                                               (gate, up)[m][:, fc, hf * HALF:(hf + 1) * HALF],
                                               AX.X, ALU.max, apply_absolute_value=True)

            def largest(n, pieces, ins):
                link(ins)
                nc.vector.tensor_reduce(amax[:, n:n + 1], part[:, n, 0:pieces], AX.X, ALU.max).then_inc(amax_ready, 1)

            for r in range(2 * FC):
                ins = largest_of_group(r)
            largest(1, 2 * FC, ins)
            scale_of(1, scl[:, 0, 1:2])
            for fc in range(FC):
                nc.vector.tensor_scalar(g_int[:, fc, :], gate[:, fc, :], scl[:, 1, 3:4], None, ALU.mult).then_inc(gint_done, 1)
            link(nc.vector.tensor_scalar(unit[:, 0:1], scl[:, 1, 1:2], 1.0 / UBITS, None, ALU.mult))
            largest_of_group(2 * FC)
            ins = largest_of_group(2 * FC + 1)
            for fc in range(FC + 1):
                if fc < FC:
                    dve.wait_ge(sint_done, fc + 1)
                    nc.vector.tensor_tensor(gate[:, fc, :], g_int[:, fc, :], s_int[:, fc, :], ALU.mult).then_inc(h_done, 1)
                if fc < FC - 1:
                    largest_of_group(2 * FC + 2 + 2 * fc)
                    ins = largest_of_group(2 * FC + 3 + 2 * fc)
                elif fc == FC - 1:
                    largest(2, 2 * FC, ins)
                if fc > 0:
                    dve.wait_ge(h_done, fc)
                    gated_max = nc.vector.tensor_reduce(part[:, 3, fc - 1:fc], gate[:, fc - 1, :], AX.X, ALU.max,
                                                        apply_absolute_value=True)
            largest(3, FC, gated_max)
            scale_of(2, scl[:, 0, 1:2])
            scale_of(3, unit[:, 0:1])
            link(nc.vector.tensor_scalar(g_int[:, 0, :], gate[:, 0, :], scl[:, 3, 3:4], None, ALU.mult))
            for fc in range(FC + 1):
                if fc < FC:
                    dve.wait_ge(uint_done, fc + 1)
                    if fc > 0:
                        dve.wait_ge(hint_done, fc)
                    nc.vector.tensor_tensor(up[:, fc, :], g_int[:, fc, :], u_int[:, fc, :], ALU.mult).then_inc(o_done, 1)
                if fc > 0:
                    dve.wait_ge(o_done, fc)
                    ins = nc.vector.tensor_reduce(part[:, 4, fc - 1:fc], up[:, fc - 1, :], AX.X, ALU.max,
                                                  apply_absolute_value=True)
            link(nc.vector.tensor_tensor(unit[:, 1:2], scl[:, 3, 1:2], scl[:, 2, 1:2], ALU.mult))
            largest(4, FC, ins)
            scale_of(4, unit[:, 1:2])
            for fc in range(FC):
                nc.vector.tensor_scalar(g_int[:, fc, :], up[:, fc, :], scl[:, 4, 3:4], None, ALU.mult).then_inc(oint_done, 1)
                dve.wait_ge(oint_done, fc + 1)
                nc.vector.tensor_copy(oq[0][:, fc, :], g_int[:, fc, :]).then_inc(o_high, 1)
                dve.wait_ge(o_high, fc + 1)
                nc.vector.tensor_tensor(oq[1][:, fc, :], g_int[:, fc, :], oq[0][:, fc, :].bitcast(F32), ALU.subtract).then_inc(o_low, 1)
            for b in range(B):
                dve.wait_ge(down_made, b + 1)
                nc.vector.scalar_tensor_tensor(out=x_sb[:, b, :], in0=bank[b][0:TQ, 0:DM], scalar=scl[0:TQ, 4, 1:2],
                                               in1=x_sb[:, b, :], op0=ALU.mult, op1=ALU.add).then_inc(y_done, 1)


def kernel(x, ctx_1024, mask_Bx1x1xS2_bk0, L0_xattn_Wq, L0_xattn_Wk, L0_xattn_Wv, L0_xattn_Wo, L0_xattn_rel_bias,
           L0_ffn_w_gate, L0_ffn_w_up, L0_ffn_w_down):
    import concourse.bacc as bacc
    from concourse.bass_utils import run_bass_kernel_spmd

    wq = np.asarray(L0_xattn_Wq).T.reshape(DM, NG, 1, GH * DK)
    onehot = np.zeros((NBUCKET, NREL), np.float32)
    for r in range(NREL):
        onehot[bucket_of(r - (TQ - 1)), r] = 1.0
    rows = np.arange(P) % (GH * DK) // DK
    padded = np.zeros((B, TKP, DM), np.float32)
    padded[:, :TK] = np.asarray(ctx_1024)
    layout = {
        "x": np.asarray(x)[:, ::-1].transpose(1, 0, 2),
        "ctxT": padded.reshape(B, TKP, KC, P).transpose(3, 0, 2, 1),
        "mask": np.asarray(mask_Bx1x1xS2_bk0).reshape(B, TK),
        "wqT": np.concatenate([wq, wq], axis=2).reshape(DM, NG, P),
        "wkT": np.asarray(L0_xattn_Wk).T,
        "wvT": np.asarray(L0_xattn_Wv).T,
        "woT": np.asarray(L0_xattn_Wo).T,
        "relT": np.asarray(L0_xattn_rel_bias).T,
        "w_gate": np.asarray(L0_ffn_w_gate),
        "w_up": np.asarray(L0_ffn_w_up),
        "w_down": np.asarray(L0_ffn_w_down),
        "onehot": onehot,
        "hmask": (rows[:, None] == np.arange(GH)[None, :]).astype(np.float32),
        "ident": np.eye(P, dtype=np.float32),
    }
    nc = bacc.Bacc("TRN2", target_bir_lowering=False, num_devices=1)
    arrays, args = {}, []
    for name, a in layout.items():
        a = np.ascontiguousarray(a)
        arrays[f"in_{name}"] = a
        args.append(nc.dram_tensor(f"in_{name}", a.shape, mybir.dt.from_np(a.dtype), kind="ExternalInput").ap())
    out = nc.dram_tensor("out_y", (TQ, B, DM), F32, kind="ExternalOutput").ap()
    build(nc, *args, out)
    r = run_bass_kernel_spmd(nc, [arrays], core_ids=[0])
    return np.ascontiguousarray(r.results[0]["out_y"].transpose(1, 0, 2)[:, ::-1])
```

```python
from contextlib import ExitStack

import numpy as np

import concourse.bass as bass
from concourse import mybir

ALU = mybir.AluOpType
ACT = mybir.ActivationFunctionType
AX = mybir.AxisListType
F32 = mybir.dt.float32
F32R = mybir.dt.float32r
BF16 = mybir.dt.bfloat16
I16 = mybir.dt.int16
U16 = mybir.dt.uint16
U8 = mybir.dt.uint8
RMAX = bass.bass_isa.ReduceOp.max

P = 128
B, TQ, TK, DM = 8, 100, 361, 256
H, DK = 16, 16
GH = 4
NG = H // GH
NI = B * NG
NH = NI * GH
KC = DM // P
NT = 3
KT = (TK + NT - 1) // NT
TKE = TK + TK % 2
TKP = NT * KT
CW = TKP + TKP % 2
CSLOTS = 3
HW = 4 * DK
PW = 2 * (HW + DK)
NTOK = B * TQ
HALF = NTOK // 2
FF = 768
FC = FF // P
WBLK = 32
NBLK = FC * DM // WBLK
NREL = TQ + TK - 1
NBUCKET = 32
MASKED = float(2.0 ** 100)
LN_EPS = 1e-5
PRODUCTS = [(0, 0), (0, 1), (1, 0)]
ACT_QMAX = 32767.0
W_QMAX = 7.0
MIN_SCALE = 1e-12
UBITS = 65536.0
ROUND = 1.5 * 2.0 ** 23

FAR_FROM = [8, 12, 16, 23, 32, 46, 64, 91]


def bucket_of(rel):
    dist = abs(rel)
    bucket = dist if dist < 8 else 7 + sum(dist >= d for d in FAR_FROM)
    return bucket + (NBUCKET // 2 if rel > 0 else 0)


def build(nc, x, ctxT, mask, wqT, wkT, wvT, woT, relT, w_gate, w_up, w_down, onehot, hmask, ident, out):
    rel_row = nc.dram_tensor("rel_row", [H, NREL], F32, kind="Internal")

    with ExitStack() as ctx:
        def sb(name, shape, dt=F32):
            return ctx.enter_context(nc.sbuf_tensor(name, shape, dt))

        def sem(name):
            return ctx.enter_context(nc.semaphore(name))

        bank = [ctx.enter_context(nc.psum_tensor(f"bank{n}", [P, 512], F32)) for n in range(8)]

        region_ctx = sb("region_ctx", [P, B * KC * TKP])
        region_bias = sb("region_bias", [P, H * TK])
        region_v = sb("region_v", [P, NI * NT * GH * DK])
        region_ffw = sb("region_ffw", [P, 3 * FC * DM])
        region_w = sb("region_w", [P, 3 * KC * DM])
        csize, wsize = CSLOTS * 2 * KC * CW, 2 * 2 * KC * DM
        region_q = sb("region_q", [P, max(2 * NI * TQ, csize + wsize)], F32R)
        region_k = sb("region_k", [P, NI * TKE], F32R)
        region_x = sb("region_x", [P, B * DM])
        region_xT = sb("region_xT", [P, KC * NTOK])
        x_sb = sb("x_sb", [TQ, B, DM])
        wo_sb = sb("wo_sb", [P, KC, DM])
        rel_sb = sb("rel_sb", [NBUCKET, H])
        hmask_sb = sb("hmask_sb", [P, GH])
        ident_sb = sb("ident_sb", [P, P])

        ctxT_sb = region_ctx[:].rearrange("p (b c n) -> p b c n", b=B, c=KC)
        wq_sb = region_w[:, 0:2 * KC * DM].rearrange("p (c g m) -> p c g m", c=KC, g=NG)
        wk_sb = region_w[:, 2 * KC * DM:].rearrange("p (c m) -> p c m", c=KC)
        wv_sb = sb("wv_sb", [P, KC, DM])
        onehot_sb = region_bias[0:NBUCKET, 0:NREL]
        mask_u8 = region_bias[0:TQ, 1024:1024 + B * TK // 4].bitcast(U8)
        ffw = region_ffw[:].rearrange("p (m n) -> p m n", m=3)
        relrow_sb = region_bias[0:H, NREL:2 * NREL]
        bias_sb = region_bias[0:TQ, :].rearrange("p (h n) -> p h n", h=H)
        mask_add = sb("mask_add", [TQ, B, TK], BF16)
        xn = region_x[0:TQ, :].rearrange("p (b d) -> p b d", b=B)
        xT = region_xT[:].rearrange("p (c n) -> p c n", c=KC)
        csplit = region_q[:, 0:csize].rearrange("p (u s c n) -> p u s c n", u=CSLOTS, s=2, c=KC)
        wksplit, wvsplit = (region_q[:, csize + m * wsize // 2:csize + (m + 1) * wsize // 2]
                            .rearrange("p (s c n) -> p s c n", s=2, c=KC) for m in range(2))
        qh, ql = (region_q[:, m * NI * TQ:(m + 1) * NI * TQ].rearrange("p (i n) -> p i n", i=NI) for m in range(2))
        kst = region_k[:].rearrange("p (i n) -> p i n", i=NI)
        v_sb = region_v[0:KT, :].rearrange("p (i t h d) -> p i t h d", i=NI, t=NT, h=GH)
        qm = sb("qm", [P, 2, 2, GH, TQ], F32R)
        v_st = region_x[0:KT, 0:NT * GH * PW].rearrange("p (u t a w) -> p u t a w", u=2, t=NT, a=GH // 2)
        mbias = region_ctx[0:TQ, 0:2 * GH * TK].rearrange("p (u h n) -> p u h n", u=2, h=GH)
        prob = region_ctx[0:TQ, 4 * KC * TKP:4 * KC * TKP + 4 * TKP].rearrange("p (s n) -> p s n", s=4)
        pT = region_w[0:KT, 0:4 * NT * TQ].rearrange("p (s n) -> p s n", s=4)
        nmax = sb("nmax", [TQ, 4])
        rsum = sb("rsum", [P, 2, TQ])
        attnT = region_xT[:].rearrange("p (s n) -> p s n", s=NI // 2)
        stats = sb("stats", [TQ, B, 6])
        mv = sb("mv", [TQ, B, 2])
        veps = sb("veps", [TQ, B])
        rstd = sb("rstd", [TQ, B])
        negmean = sb("negmean", [TQ, B])
        mhalf = sb("mhalf", [TQ, B])
        wmax = sb("wmax", [P, 3, NBLK])
        wscale = sb("wscale", [P, 3, NBLK])
        winv = sb("winv", [P, 3, NBLK])
        part = sb("part", [P, 5, 2 * FC])
        amax = sb("amax", [P, 5])
        gmax = sb("gmax", [P, 5])
        scl = sb("scl", [P, 5, 4])
        unit = sb("unit", [P, 2])
        wT = region_k[:, 0:6 * FC * DM].rearrange("p (m s n) -> p m s n", m=3, s=2)
        xq = region_q[:, 0:2 * KC * NTOK].rearrange("p (s k n) -> p s k n", s=2, k=KC)
        oq = [t[:, 0:FC * NTOK].rearrange("p (k n) -> p k n", k=FC) for t in (region_q, region_k)]
        gate, up = (t[:, 0:FC * NTOK].rearrange("p (c n) -> p c n", c=FC) for t in (region_ctx, region_bias))
        g_int, u_int = (region_v[:, m * FC * NTOK // 2:(m + 1) * FC * NTOK // 2].bitcast(I16).rearrange("p (c n) -> p c n", c=FC)
                        for m in range(2))
        s_int = region_ffw[:, 0:FC * NTOK // 2].bitcast(U16).rearrange("p (c n) -> p c n", c=FC)
        x_int = region_w[:, 0:KC * NTOK // 2].bitcast(I16).rearrange("p (c n) -> p c n", c=KC)

        loaded = {n: sem(f"loaded_{n}") for n in ("x", "wq", "wk", "wv", "wo", "const", "mask", "ffw")}
        ctx_loaded = [sem(f"ctx_loaded{b}") for b in range(B)]
        relrow_stored, bias_loaded, out_stored = sem("relrow_stored"), sem("bias_loaded"), sem("out_stored")
        dve_step, pool_step = sem("dve_step"), sem("pool_step")
        ln_var, ln_rstd, ln_mean = sem("ln_var"), sem("ln_rstd"), sem("ln_mean")
        xn_even, xn_odd = sem("xn_even"), sem("xn_odd")
        winv_done, wdiv_done, wround_done, ffw_done = sem("winv_done"), sem("wdiv_done"), sem("wround_done"), sem("ffw_done")
        fill_done, mask_done = sem("fill_done"), sem("mask_done")
        pad_done = sem("pad_done")
        wkv_high, wkv_low, ctx_high, ctx_low = sem("wkv_high"), sem("wkv_low"), sem("ctx_high"), sem("ctx_low")
        job_done, act_evac, dve_evac = sem("job_done"), sem("act_evac"), sem("dve_evac")
        qm_high, qm_low, bias_ready, v_ready = sem("qm_high"), sem("qm_low"), sem("bias_ready"), sem("v_ready")
        scores_ready, z_done, prob_ready, t_ready = sem("scores_ready"), sem("z_done"), sem("prob_ready"), sem("t_ready")
        pt_ready = sem("pt_ready")
        o_ready, rsum_done, attn_done = sem("o_ready"), sem("rsum_done"), sem("attn_done")
        wo_made, res_done = sem("wo_made"), sem("res_done")
        w_turned, w_high, w_low = sem("w_turned"), sem("w_high"), sem("w_low")
        x_turned, xint_act, xint_dve = sem("x_turned"), sem("xint_act"), sem("xint_dve")
        x_high, x_low = sem("x_high"), sem("x_low")
        amax_ready, gmax_ready, scale_ready = sem("amax_ready"), sem("gmax_ready"), sem("scale_ready")
        gu_made, gu_copied = sem("gu_made"), sem("gu_copied")
        gint_done = sem("gint_done")
        sig_done, sint_done, h_done = sem("sig_done"), sem("sint_done"), sem("h_done")
        uint_done, hint_done, o_done = sem("uint_done"), sem("hint_done"), sem("o_done")
        oint_done, o_high, o_low = sem("oint_done"), sem("o_high"), sem("o_low")
        down_made, y_done = sem("down_made"), sem("y_done")

        XT_BEFORE = 6
        def of_batch(b):
            return [("k", b, m) for m in range(KC)] + [("v", b, t) for t in range(NT)]

        jobs = []
        for b in range(B):
            if b == XT_BEFORE:
                jobs += [("xT", c, 0) for c in range(B // 2)]
            jobs += of_batch(b)
            if b == 0:
                jobs += [("rel", 0, 0)]
        jobs += [("q", g, hf) for hf in range(2) for g in range(NG)]

        def on_dve(n):
            return jobs[n][0] in ("q", "k")

        def dve_after(n):
            return sum(on_dve(m) for m in range(n + 1))

        def bank_free(eng, n):
            if n >= 8:
                eng.wait_ge(act_evac, n - 7)
                if on_dve(n - 8):
                    eng.wait_ge(dve_evac, dve_after(n - 8))

        first_job, last_job = {}, {}
        for n, (kind, _, _) in enumerate(jobs):
            first_job.setdefault(kind, n)
            last_job[kind] = n
        first_q = jobs.index(("q", NG - 1, 0))

        WGROUPS = 9
        W_GATE, W_UP = 3, 6
        GROUPS = 4 * FC


        def bank_of(r):
            return bank[(0, 1, 2, 3, 5, 6, 7, 4)[r % 8]]

        def group(r):
            return r // (2 * FC), r // FC % 2, r % FC

        FILLS = 7
        TOKENS_AFTER = 4
        SCALES_AFTER, ROUND_AFTER = (1, 2, 3), (5, 6, 7)

        block = ctx.enter_context(nc.Block())

        @block.sync
        def _(sp):
            sp.dma_start(wk_sb, wkT.rearrange("(c p) m -> p c m", p=P)).then_inc(loaded["wk"], 16)
            for b in range(B):
                sp.dma_start(ctxT_sb[:, b], ctxT[:, b]).then_inc(ctx_loaded[b], 16)
                if b == 0:
                    sp.dma_start(onehot_sb[:], onehot).then_inc(loaded["const"], 16)
                    sp.dma_start(rel_sb[:], relT).then_inc(loaded["const"], 16)
                if b == 1:
                    sp.dma_start(x_sb[:], x).then_inc(loaded["x"], 16)
                if 2 <= b < 5:
                    slabs = (FC, FC, KC)[b - 2]
                    sp.dma_start(ffw[:, b - 2, :].rearrange("p (c i) -> p c i", c=slabs),
                                 (w_gate, w_up, w_down)[b - 2].rearrange("(c p) i -> p c i", p=P)).then_inc(loaded["ffw"], 16)
                if b == 5:
                    sp.dma_start(wq_sb, wqT.rearrange("(c p) g m -> p c g m", p=P)).then_inc(loaded["wq"], 16)
            sp.dma_start(wo_sb[:], woT.rearrange("(c p) m -> p c m", p=P)).then_inc(loaded["wo"], 16)
            sp.wait_ge(act_evac, first_job["rel"] + 1)
            sp.dma_start(rel_row.ap(), relrow_sb[:]).then_inc(relrow_stored, 16)
            sp.wait_ge(relrow_stored, 16)
            sp.wait_ge(mask_done, 1)
            window = bass.AP(rel_row, 0, [[1, TQ], [NREL, H], [1, TK]])
            sp.dma_start(bias_sb[:], window).then_inc(bias_loaded, 16)
            for c in range(B // 2):
                sp.wait_ge(y_done, 2 * c + 2)
                sp.dma_start(out[:, 2 * c:2 * c + 2, :], x_sb[:, 2 * c:2 * c + 2, :]).then_inc(out_stored, 16)
            sp.wait_ge(out_stored, 16 * (B // 2))

        def turned(c):
            return bank[c][:, 0:4 * TQ].rearrange("p (k n) -> p k n", k=KC)

        def of_tokens(t, c):
            return t[:, :, 2 * c * TQ:2 * (c + 1) * TQ]

        @block.gpsimd
        def _(pool):
            steps = [0]

            def link(ins):
                steps[0] += 1
                ins.then_inc(pool_step, 1)
                pool.wait_ge(pool_step, steps[0])

            pool.dma_start(mask_u8, mask.rearrange("b n -> (b n)").partition_broadcast(TQ)).then_inc(loaded["mask"], 16)
            nc.gpsimd.memset(mhalf[:], -0.5).then_inc(fill_done, 1)
            nc.gpsimd.memset(kst[:, :, TK:].bitcast(F32), 0.0).then_inc(fill_done, 1)
            nc.gpsimd.memset(amax[:], 0.0).then_inc(fill_done, 1)
            def normalize_tokens(c, n):
                bs, b = slice(2 * c, 2 * c + 2), 2 * c + 1
                pool.wait_ge(ln_var, n)
                link(nc.gpsimd.tensor_scalar(veps[:, bs], mv[:, bs, 1], LN_EPS, None, ALU.add))
                nc.gpsimd.tensor_tensor(rstd[:, bs], veps[:, bs], mhalf[:, bs], ALU.pow).then_inc(ln_rstd, 1)
                nc.gpsimd.tensor_scalar(negmean[:, b:b + 1], mv[:, b, 0:1], -1.0, None, ALU.mult).then_inc(ln_mean, 1)
                pool.wait_ge(ln_rstd, n)
                pool.wait_ge(ln_mean, n)
                nc.gpsimd.tensor_scalar(xn[:, b, :], x_sb[:, b, :], negmean[:, b:b + 1], rstd[:, b:b + 1],
                                        ALU.add, ALU.mult).then_inc(xn_odd, 1)

            def context_low(b):
                pool.wait_ge(ctx_high, b + 1)
                nc.gpsimd.tensor_tensor(csplit[:, b % CSLOTS, 1, :, 0:TKP], ctxT_sb[:, b],
                                        csplit[:, b % CSLOTS, 0, :, 0:TKP].bitcast(F32), ALU.subtract).then_inc(ctx_low, 1)

            for b in range(CSLOTS):
                context_low(b)
            context_low(CSLOTS)
            normalize_tokens(0, 1)
            normalize_tokens(1, 2)
            context_low(CSLOTS + 1)
            normalize_tokens(2, 3)
            normalize_tokens(3, 4)

            def select_heads(g, i):
                pool.wait_ge(loaded["const"], 64)
                if not (isinstance(i, int) and i < 2):
                    pool.wait_ge(scores_ready, i * GH - GH)
                nc.gpsimd.tensor_tensor(
                    qm[:, g % 2, 0], qh[:, bass.ds(i, 1), :].bitcast(F32).to_broadcast([P, GH, TQ]),
                    hmask_sb[:].unsqueeze(2).to_broadcast([P, GH, TQ]), ALU.mult).then_inc(qm_high, 1)

            def add_mask(b, g, i):
                for h in (0, GH // 2):
                    taken = i * GH - 2 * GH + h + GH // 2
                    if not isinstance(i, int):
                        taken = pool.to_reg(taken)
                    pool.wait_ge(mask_done, 1)
                    if not (isinstance(i, int) and i < 2):
                        pool.wait_ge(z_done, taken)
                    nc.gpsimd.tensor_tensor(
                        mbias[:, g % 2, h:h + GH // 2], bias_sb[:, g * GH + h:g * GH + h + GH // 2, :],
                        mask_add[:, bass.ds(b, 1), :].to_broadcast([TQ, GH // 2, TK]), ALU.add).then_inc(bias_ready, 1)

            def blocks(m):
                return ffw[:, m, :].rearrange("p (n k) -> p n k", k=WBLK)

            for m in range(3):
                context_low(CSLOTS + 2 + m)
                pool.wait_ge(winv_done, m + 1)
                nc.gpsimd.tensor_tensor(blocks(m), blocks(m), winv[:, m, :].unsqueeze(2).to_broadcast([P, NBLK, WBLK]),
                                        ALU.mult).then_inc(wdiv_done, 1)
            def scale_weights(m):
                pool.wait_ge(wround_done, m + 1)
                nc.gpsimd.tensor_tensor(blocks(m), blocks(m), wscale[:, m, :].unsqueeze(2).to_broadcast([P, NBLK, WBLK]),
                                        ALU.mult).then_inc(ffw_done, 1)

            scale_weights(0)
            pool.wait_ge(ctx_high, B)
            pool.wait_ge(ctx_low, B)
            pool.wait_ge(bias_loaded, 16)
            add_mask(0, 0, 0)
            pool.wait_ge(act_evac, first_q + 1)
            pool.wait_ge(dve_evac, dve_after(first_q))
            for g in range(NG):
                select_heads(g, g)
                if g >= 1:
                    add_mask(0, g, g)
            pool.wait_ge(act_evac, last_job["q"] + 1)
            pool.wait_ge(dve_evac, dve_after(last_job["q"]))
            with nc.gpsimd.Fori(1, B) as b:
                for g in range(NG):
                    select_heads(g, b * NG + g)
                    add_mask(b, g, b * NG + g)

            scale_weights(1)
            scale_weights(2)
            for c in range(B // 2):
                normalize_tokens(c, B // 2 + c + 1)

            def over_partitions(n):
                pool.wait_ge(amax_ready, n + 1)
                nc.gpsimd.partition_all_reduce(gmax[:, n:n + 1], amax[:, n:n + 1], P, RMAX).then_inc(gmax_ready, 1)

            over_partitions(0)
            over_partitions(1)
            over_partitions(2)
            over_partitions(3)
            over_partitions(4)

        @block.tensor
        def _(pe):
            for n, (kind, a, c) in enumerate(jobs):
                bk = bank[n % 8]
                bank_free(pe, n)
                if kind == "rel":
                    pe.wait_ge(loaded["const"], 64)
                    mm = nc.tensor.matmul(bk[0:H, 0:NREL], rel_sb[:], onehot_sb[:], start=True, stop=True)
                elif kind == "xT":
                    pe.wait_ge(xn_even, a + 1)
                    pe.wait_ge(xn_odd, a + 1)
                    for j in range(2):
                        for k in range(KC):
                            mm = nc.tensor.transpose(bk[:, (2 * k + j) * TQ:(2 * k + j + 1) * TQ],
                                                     xn[:, 2 * a + j, k * P:(k + 1) * P], ident_sb[0:TQ, 0:TQ])
                elif kind == "q":
                    if n == first_job["q"]:
                        pe.wait_ge(loaded["wq"], 16)
                        pe.wait_ge(act_evac, last_job["xT"] + 1)
                    for k in range(KC):
                        mm = nc.tensor.matmul(bk[:, 0:HALF], wq_sb[:, k, a, :], xT[:, k, c * HALF:(c + 1) * HALF],
                                              start=(k == 0), stop=(k == KC - 1))
                elif kind == "k":
                    if n == first_job["k"]:
                        pe.wait_ge(wkv_low, 2)
                    if c == 0:
                        pe.wait_ge(ctx_low, a + 1)
                    for ws, xs in PRODUCTS:
                        for k in range(KC):
                            mm = nc.tensor.matmul(bk[:, 0:TKE], wksplit[:, ws, k, c * P:(c + 1) * P],
                                                  csplit[:, a % CSLOTS, xs, k, 0:TKE], start=(k == 0 and (ws, xs) == PRODUCTS[0]),
                                                  stop=(k == KC - 1 and (ws, xs) == PRODUCTS[-1]))
                elif kind == "v":
                    for ws, xs in PRODUCTS:
                        for k in range(KC):
                            mm = nc.tensor.matmul(bk[0:KT, 0:DM], csplit[:, a % CSLOTS, xs, k, c * KT:(c + 1) * KT],
                                                  wvsplit[:, ws, k, :], start=(k == 0 and (ws, xs) == PRODUCTS[0]),
                                                  stop=(k == KC - 1 and (ws, xs) == PRODUCTS[-1]))
                mm.then_inc(job_done, 1)

            pe.wait_ge(act_evac, len(jobs))
            pe.wait_ge(dve_evac, dve_after(len(jobs) - 1))

            def scores(step2, j, m, i, first):
                bk = bank[j % 4]
                u = (j // GH) % 2
                if j % GH == 0:
                    pe.wait_ge(qm_high, i + 1)
                    pe.wait_ge(qm_low, i + 1)
                if not first:
                    pe.wait_ge(z_done, m - 3)
                for part_no in range(2):
                    mm = nc.tensor.matmul(bk[0:TQ, 0:TKE], qm[:, u, part_no, j % GH, :],
                                          kst[:, bass.ds(i, 1), :].rearrange("p a n -> p (a n)"),
                                          start=(part_no == 0), stop=(part_no == 1))
                mm.then_inc(scores_ready, 1)

            def weigh(p, j):
                i = p * 2 + j // GH
                u, pair, second = j // GH, j % GH // 2, j % 2
                o = bank[6 + u][pair * HW:(pair + 1) * HW, 0:TQ]
                pe.wait_ge(pt_ready, p * 8 + j + 1)
                if j % GH == 0:
                    pe.wait_ge(v_ready, i + 1)
                    if not (isinstance(i, int) and i < 2):
                        pe.wait_ge(attn_done, i - 1)
                for t in range(NT):
                    mm = nc.tensor.matmul(o, v_st[:, u, t, pair, second * HW:(second + 1) * HW],
                                          pT[:, j % 4, t * TQ:(t + 1) * TQ],
                                          start=(not second and t == 0), stop=(bool(second) and t == NT - 1))
                mm.then_inc(o_ready, 1)

            def two_steps(p, last):
                static = isinstance(p, int)
                for j in range(8):
                    if not (last and j + 3 >= 8):
                        m = p * 8 + (j + 3)
                        jj = (j + 3) % 8
                        scores(None, jj, m, p * 2 + (j + 3) // GH, static and m < 4)
                    n = p * 8 + j
                    bk = bank[4 + j % 2]
                    pe.wait_ge(prob_ready, n + 1)
                    if not (static and n < 2):
                        pe.wait_ge(pt_ready, n - 1)
                    for t in range(NT):
                        mm = nc.tensor.transpose(bk[0:KT, t * TQ:(t + 1) * TQ], prob[:, j % 4, t * KT:(t + 1) * KT],
                                                 ident_sb[0:TQ, 0:TQ])
                    mm.then_inc(t_ready, 1)
                    if j > 0:
                        weigh(p, j - 1)
                    elif not (static and p == 0):
                        weigh(p - 1, 7)

            pe.wait_ge(fill_done, FILLS)
            pe.wait_ge(pad_done, 1)
            for m in range(3):
                scores(None, m, m, 0, True)
            two_steps(0, False)
            with nc.tensor.Fori(1, NI // 2 - 1) as p:
                two_steps(p, False)
            two_steps(NI // 2 - 1, True)
            weigh(NI // 2 - 1, 7)

            def turn_weights(r):
                m, c = r // 3, r % 3
                bk = bank[4 + r % 4]
                pe.wait_ge(ffw_done, m + 1)
                if r >= 4:
                    pe.wait_ge(w_low, r - 3)
                for j in range(4):
                    n = 4 * c + j
                    at = (n % FC) * DM + (n // FC) * P if m < 2 else (n % KC) * FF + (n // KC) * P
                    mm = nc.tensor.transpose(bk[:, j * P:(j + 1) * P], ffw[:, m, at:at + P], ident_sb[:])
                mm.then_inc(w_turned, 1)

            pe.wait_ge(pt_ready, NH)
            pe.wait_ge(z_done, NH)
            turn_weights(0)
            turn_weights(1)
            pe.wait_ge(loaded["wo"], 16)
            for c in range(B // 2):
                pe.wait_ge(attn_done, 2 * NG * (c + 1))
                for j in range(2):
                    for k in range(KC):
                        mm = nc.tensor.matmul(bank[c][0:TQ, j * DM:(j + 1) * DM], attnT[:, (2 * c + j) * KC + k, :],
                                              wo_sb[:, k, :], start=(k == 0), stop=(k == KC - 1))
                mm.then_inc(wo_made, 1)
            for r in range(2, 6):
                turn_weights(r)
            for c in range(B // 2):
                pe.wait_ge(res_done, c + 1)
                pe.wait_ge(xn_even, B // 2 + c + 1)
                pe.wait_ge(xn_odd, B // 2 + c + 1)
                for j in range(2):
                    for k in range(KC):
                        mm = nc.tensor.transpose(bank[c][:, (2 * k + j) * TQ:(2 * k + j + 1) * TQ],
                                                 xn[:, 2 * c + j, k * P:(k + 1) * P], ident_sb[0:TQ, 0:TQ])
                mm.then_inc(x_turned, 1)
            turn_weights(6)
            turn_weights(7)
            pe.wait_ge(w_low, W_GATE)
            for r in range(GROUPS):
                m, hf, fc = group(r)
                if fc == 0 and m == 0:
                    pe.wait_ge(x_low, B // 4 * (hf + 1))
                if r == 2:
                    turn_weights(WGROUPS - 1)
                if r in (4, 7):
                    pe.wait_ge(w_low, WGROUPS - (r == 4))
                if r >= 8:
                    pe.wait_ge(gu_copied, r - 7)
                for k in range(KC):
                    for ws, xs in PRODUCTS:
                        mm = nc.tensor.matmul(bank_of(r)[:, 0:HALF], wT[:, m, ws, k * FF + fc * P:k * FF + (fc + 1) * P],
                                              xq[:, xs, k, hf * HALF:(hf + 1) * HALF], start=(k == 0 and (ws, xs) == PRODUCTS[0]),
                                              stop=(k == KC - 1 and (ws, xs) == PRODUCTS[-1]))
                mm.then_inc(gu_made, 1)

            def down(b, k, ws, xs):
                first, final = (k == 0 and (ws, xs) == PRODUCTS[0]), (k == FC - 1 and (ws, xs) == (0, 1))
                return nc.tensor.matmul(bank[b][0:TQ, 0:DM], oq[xs][:, k, b * TQ:(b + 1) * TQ],
                                        wT[:, 2, ws, k * DM:(k + 1) * DM], start=first, stop=final)

            pe.wait_ge(gu_copied, GROUPS)
            for k in range(FC - 1):
                pe.wait_ge(o_high, k + 1)
                for b in range(B):
                    down(b, k, 0, 0)
                    down(b, k, 1, 0)
                pe.wait_ge(o_low, k + 1)
                for b in range(B):
                    down(b, k, 0, 1)
            pe.wait_ge(o_low, FC)
            for b in range(B):
                down(b, FC - 1, 0, 0)
                down(b, FC - 1, 1, 0)
                down(b, FC - 1, 0, 1).then_inc(down_made, 1)

        @block.scalar
        def _(act):
            act.dma_start(wv_sb[:], wvT.rearrange("(c p) m -> p c m", p=P)).then_inc(loaded["wv"], 16)
            act.dma_start(ident_sb[:], ident).then_inc(loaded["const"], 16)
            act.dma_start(hmask_sb[:], hmask).then_inc(loaded["const"], 16)
            def context_high(b):
                act.wait_ge(ctx_loaded[b], 16)
                nc.scalar.copy(csplit[:, b % CSLOTS, 0, :, 0:TKP], ctxT_sb[:, b]).then_inc(ctx_high, 1)

            act.wait_ge(loaded["wk"], 16)
            nc.scalar.copy(wksplit[:, 0], wk_sb).then_inc(wkv_high, 1)
            context_high(0)
            act.wait_ge(loaded["wv"], 16)
            nc.scalar.copy(wvsplit[:, 0], wv_sb[:]).then_inc(wkv_high, 1)
            for b in range(1, CSLOTS):
                context_high(b)
            for n, (kind, a, c) in enumerate(jobs):
                bk = bank[n % 8]
                act.wait_ge(job_done, n + 1)
                if kind == "rel":
                    ins = nc.scalar.copy(relrow_sb[:], bk[0:H, 0:NREL])
                elif kind == "xT":
                    ins = nc.scalar.copy(xT[:, :, 2 * a * TQ:2 * (a + 1) * TQ],
                                         bk[:, 0:4 * TQ].rearrange("p (k n) -> p k n", k=KC))
                elif kind == "q":
                    ins = nc.scalar.copy(
                        qh[:].rearrange("p (b g) q -> p b g q", g=NG)[:, c * B // 2:(c + 1) * B // 2, a, :],
                        bk[:, 0:HALF].rearrange("p (b q) -> p b q", q=TQ))
                elif kind == "k":
                    nc.scalar.copy(kst[0:64, a * NG + 2 * c, 0:TK], bk[0:64, 0:TK])
                    ins = nc.scalar.copy(kst[64:P, a * NG + 2 * c + 1, 0:TK], bk[64:P, 0:TK])
                else:
                    ins = nc.scalar.copy(v_sb[:, a * NG:(a + 1) * NG, c],
                                         bk[0:KT, 0:DM].rearrange("p (g h d) -> p g h d", g=NG, h=GH))
                ins.then_inc(act_evac, 1)
                if kind == "rel":
                    act.wait_ge(loaded["mask"], 16)
                    nc.scalar.activation(mask_add[:].rearrange("p b n -> p (b n)"), mask_u8, ACT.Copy, bias=-MASKED,
                                         scale=MASKED).then_inc(mask_done, 1)
                if (kind, c) == ("v", NT - 1) and a + CSLOTS < B:
                    context_high(a + CSLOTS)

            def stage_values(i, u):
                if not (isinstance(i, int) and i < 2):
                    act.wait_ge(o_ready, i * GH - GH)
                nc.scalar.copy(v_st[:, u].rearrange("p t a (c w) -> p (t a) c w", c=2)[:, :, :, 0:DK],
                               v_sb[:, bass.ds(i, 1)].rearrange("p i t (a c) d -> p (i t a) c d", c=2)).then_inc(v_ready, 1)

            def exponent(p, j, m):
                act.wait_ge(z_done, m + 1)
                nc.scalar.activation(prob[:, j % 4, 0:TK], prob[:, j % 4, 0:TK], ACT.Exp, bias=nmax[:, j % 4:j % 4 + 1],
                                     scale=-1.0).then_inc(prob_ready, 1)

            def two_steps(p, last):
                for j in range(8):
                    n = p * 8 + j
                    if not (last and j == 7):
                        exponent(p, (j + 1) % 8, n + 1)
                    act.wait_ge(t_ready, n + 1)
                    if not (isinstance(n, int) and n < 4):
                        act.wait_ge(o_ready, n - 3)
                    nc.scalar.copy(pT[:, j % 4, :], bank[4 + j % 2][0:KT, 0:NT * TQ]).then_inc(pt_ready, 1)
                    if j == 1:
                        stage_values(p * 2 + 1, 1)
                    if j == 5 and not last:
                        stage_values(p * 2 + 2, 0)

            act.wait_ge(fill_done, FILLS)
            act.wait_ge(act_evac, len(jobs))
            stage_values(0, 0)
            exponent(0, 0, 0)
            two_steps(0, False)
            with nc.scalar.Fori(1, NI // 2 - 1) as p:
                two_steps(p, False)
            two_steps(NI // 2 - 1, True)

            def weights_high(r):
                act.wait_ge(w_turned, r + 1)
                nc.scalar.copy(wT[:, r // 3, 0, r % 3 * 512:(r % 3 + 1) * 512], bank[4 + r % 4][:]).then_inc(w_high, 1)

            for r in range(6):
                weights_high(r)
            act.wait_ge(scale_ready, 1)
            for c in range(B // 4):
                act.wait_ge(x_turned, c + 1)
                nc.scalar.activation(of_tokens(x_int, c), turned(c), ACT.Copy, scale=scl[:, 0, 2:3]).then_inc(xint_act, 1)
            for c in range(B // 2):
                if c < B // 4:
                    act.wait_ge(xint_act, c + 1)
                else:
                    act.wait_ge(xint_dve, c - B // 4 + 1)
                nc.scalar.copy(of_tokens(xq[:, 0], c), of_tokens(x_int, c)).then_inc(x_high, 1)
            for r in range(6, WGROUPS):
                weights_high(r)

            def copy_group(r):
                m, hf, fc = group(r)
                act.wait_ge(gu_made, r + 1)
                nc.scalar.copy((gate, up)[m][:, fc, hf * HALF:(hf + 1) * HALF], bank_of(r)[:, 0:HALF]).then_inc(gu_copied, 1)

            for r in range(2 * FC + 2):
                copy_group(r)
            act.wait_ge(scale_ready, 2)
            for fc in range(FC):
                act.wait_ge(gint_done, fc + 1)
                nc.scalar.activation(gate[:, fc, :], g_int[:, fc, :], ACT.Sigmoid, scale=scl[:, 1, 1:2]).then_inc(sig_done, 1)
                if fc < FC - 1:
                    copy_group(2 * FC + 2 + 2 * fc)
                act.wait_ge(sig_done, fc + 1)
                nc.scalar.activation(s_int[:, fc, :], gate[:, fc, :], ACT.Copy, scale=UBITS).then_inc(sint_done, 1)
                if fc < FC - 1:
                    copy_group(2 * FC + 3 + 2 * fc)
            act.wait_ge(scale_ready, 3)
            for fc in range(FC):
                nc.scalar.activation(u_int[:, fc, :], up[:, fc, :], ACT.Copy, scale=scl[:, 2, 3:4]).then_inc(uint_done, 1)
                if fc > 0:
                    act.wait_ge(scale_ready, 4)
                    nc.scalar.activation(g_int[:, fc, :], gate[:, fc, :], ACT.Copy, scale=scl[:, 3, 3:4]).then_inc(hint_done, 1)

        @block.vector
        def _(dve):
            steps = [0]

            def link(ins):
                steps[0] += 1
                ins.then_inc(dve_step, 1)
                dve.wait_ge(dve_step, steps[0])

            def variance(c):
                for b in (2 * c, 2 * c + 1):
                    ins = nc.vector.bn_stats(stats[:, b, :], x_sb[:, b, :])
                link(ins)
                for b in (2 * c, 2 * c + 1):
                    ins = nc.vector.bn_aggr(mv[:, b, :], stats[:, b, :])
                ins.then_inc(ln_var, 1)

            def normalize_tokens(c, n):
                dve.wait_ge(ln_rstd, n)
                nc.vector.tensor_scalar(xn[:, 2 * c, :], x_sb[:, 2 * c, :], mv[:, 2 * c, 0:1], rstd[:, 2 * c:2 * c + 1],
                                        ALU.subtract, ALU.mult).then_inc(xn_even, 1)

            def weight_scales(m):
                link(nc.vector.tensor_reduce(wmax[:, m, :], ffw[:, m, :].rearrange("p (n k) -> p n k", k=WBLK), AX.X, ALU.max,
                                             apply_absolute_value=True))
                link(nc.vector.tensor_scalar(wscale[:, m, :], wmax[:, m, :], 1.0 / W_QMAX, MIN_SCALE, ALU.mult, ALU.max))
                nc.vector.reciprocal(winv[:, m, :], wscale[:, m, :]).then_inc(winv_done, 1)

            def round_weights(m):
                dve.wait_ge(wdiv_done, m + 1)
                link(nc.vector.tensor_scalar(ffw[:, m, :], ffw[:, m, :], ROUND, -ROUND, ALU.add, ALU.add))
                nc.vector.tensor_scalar(ffw[:, m, :], ffw[:, m, :], W_QMAX, -W_QMAX - 1.0, ALU.min, ALU.max).then_inc(wround_done, 1)

            for m, (w, split) in enumerate(((wk_sb, wksplit), (wv_sb[:], wvsplit))):
                dve.wait_ge(wkv_high, m + 1)
                nc.vector.tensor_tensor(split[:, 1], w, split[:, 0].bitcast(F32), ALU.subtract).then_inc(wkv_low, 1)
            dve.wait_ge(loaded["x"], 16)
            for c in range(B // 2):
                variance(c)
            def mask_low(i, u):
                if not (isinstance(i, int) and i < 2):
                    dve.wait_ge(scores_ready, i * GH - GH)
                for h in range(GH):
                    ins = nc.vector.tensor_scalar(qm[:, u, 1, h, :], ql[:, bass.ds(i, 1), :].rearrange("p a n -> p (a n)").bitcast(F32),
                                                  hmask_sb[:, h:h + 1], None, ALU.mult)
                ins.then_inc(qm_low, 1)

            def fill():
                dve.wait_ge(job_done, last_job["xT"] + 1)
                pairs = v_st[:].rearrange("p u t a w -> p (u t a) w")
                for at, n, value in ((0, 2 * DK, 0.0), (2 * DK, DK, 1.0), (3 * DK, HW, 0.0), (HW + 3 * DK, DK, 1.0)):
                    nc.vector.memset(pairs[:, :, at:at + n], value).then_inc(fill_done, 1)
                dve.wait_ge(ctx_high, B)
                dve.wait_ge(ctx_low, B)
                nc.vector.memset(prob[:, :, TK:], 0.0).then_inc(pad_done, 1)

            for n, (kind, a, c) in enumerate(jobs):
                if not on_dve(n):
                    continue
                bk = bank[n % 8]
                dve.wait_ge(act_evac, n + 1)
                if kind == "q":
                    part_of = [t[:].rearrange("p (b g) q -> p b g q", g=NG)[:, c * B // 2:(c + 1) * B // 2, a, :] for t in (qh, ql)]
                    ins = nc.vector.tensor_tensor(part_of[1], bk[:, 0:HALF].rearrange("p (b q) -> p b q", q=TQ),
                                                  part_of[0].bitcast(F32), ALU.subtract)
                else:
                    lo, hi = kst[64:P, a * NG + 2 * c, 0:TK], kst[0:64, a * NG + 2 * c, 0:TK]
                    nc.vector.tensor_tensor(lo, bk[0:64, 0:TK], hi.bitcast(F32), ALU.subtract)
                    lo, hi = kst[0:64, a * NG + 2 * c + 1, 0:TK], kst[64:P, a * NG + 2 * c + 1, 0:TK]
                    ins = nc.vector.tensor_tensor(lo, bk[64:P, 0:TK], hi.bitcast(F32), ALU.subtract)
                ins.then_inc(dve_evac, 1)
                if n == first_q:
                    dve.wait_ge(dve_evac, dve_after(n))
                    dve.wait_ge(loaded["const"], 64)
                    mask_low(0, 0)
                    mask_low(1, 1)
                if (kind, c) == ("k", KC - 1):
                    if a == TOKENS_AFTER:
                        for pair in range(B // 2):
                            normalize_tokens(pair, pair + 1)
                    if a in SCALES_AFTER:
                        dve.wait_ge(loaded["ffw"], 48)
                        weight_scales(SCALES_AFTER.index(a))
                    if a in ROUND_AFTER:
                        round_weights(ROUND_AFTER.index(a))
                    if a == B - 1:
                        fill()

            def biased(j, m, i):
                if j % 2 == 0:
                    dve.wait_ge(bias_ready, i * 2 + j % GH // 2 + 1)
                if not (isinstance(m, int) and m < 4):
                    dve.wait_ge(t_ready, m - 3)
                made = m + 1 if isinstance(m, int) else dve.to_reg(m + 1)
                dve.wait_ge(pad_done, 1)
                dve.wait_ge(scores_ready, made)
                nc.vector.tensor_tensor_reduce(
                    out=prob[:, j % 4, 0:TK], in0=bank[j % 4][0:TQ, 0:TK], in1=mbias[:, (j // GH) % 2, j % GH, :],
                    scale=-1.0, scalar=3.0e38, op0=ALU.add, op1=ALU.min,
                    accum_out=nmax[:, j % 4:j % 4 + 1]).then_inc(z_done, 1)

            def invert_sums(i, u):
                dve.wait_ge(o_ready, i * GH + GH)
                o = bank[6 + u]
                nc.vector.reciprocal(rsum[:, u, :], o[:, 0:TQ]).then_inc(rsum_done, 1)

            def normalize(i, u, s):
                o = bank[6 + u]
                dve.wait_ge(rsum_done, i + 1)
                for pair in range(2):
                    values, sums = pair * HW, pair * HW + 2 * DK
                    rows = (2 * u + pair) * 2 * DK
                    ins = nc.vector.tensor_tensor(
                        attnT[rows:rows + 2 * DK, bass.ds(s, 1), :].rearrange("p a n -> p (a n)"), o[values:values + 2 * DK, 0:TQ],
                        rsum[sums:sums + 2 * DK, u, :], ALU.mult)
                ins.then_inc(attn_done, 1)

            def two_steps(p, last):
                for j in range(8):
                    if not (last and j + 2 >= 8):
                        biased((j + 2) % 8, p * 8 + j + 2, p * 2 + (j + 2) // GH)
                    if j % GH == 1 and not last:
                        mask_low(p * 2 + 2 + j // GH, j // GH)
                    if j % GH >= 2 and not (isinstance(p, int) and p == 0 and j < GH):
                        if j % GH == 2:
                            invert_sums(p * 2 + j // GH - 1, 1 - j // GH)
                        else:
                            normalize(p * 2 + j // GH - 1, 1 - j // GH, p + j // GH - 1)

            dve.wait_ge(dve_evac, dve_after(len(jobs) - 1))
            biased(0, 0, 0)
            biased(1, 1, 0)
            two_steps(0, False)
            with nc.vector.Fori(1, NI // 2 - 1) as p:
                two_steps(p, False)
            two_steps(NI // 2 - 1, True)
            invert_sums(NI - 1, 1)
            normalize(NI - 1, 1, NI // 2 - 1)

            def weights_low(r):
                dve.wait_ge(w_high, r + 1)
                wcols = slice(r % 3 * 512, (r % 3 + 1) * 512)
                nc.vector.tensor_tensor(wT[:, r // 3, 1, wcols], bank[4 + r % 4][:], wT[:, r // 3, 0, wcols].bitcast(F32),
                                        ALU.subtract).then_inc(w_low, 1)

            def largest_tokens(c):
                dve.wait_ge(xn_even, B // 2 + c + 1)
                dve.wait_ge(xn_odd, B // 2 + c + 1)
                return nc.vector.tensor_reduce(part[0:TQ, 0, c:c + 1], xn[:, 2 * c:2 * c + 2, :], AX.XY, ALU.max,
                                               apply_absolute_value=True)

            weights_low(0)
            weights_low(1)
            for c in range(B // 2):
                dve.wait_ge(wo_made, c + 1)
                pair = x_sb[:, 2 * c:2 * c + 2, :]
                nc.vector.tensor_tensor(pair, bank[c][0:TQ, :].rearrange("p (j d) -> p j d", j=2), pair,
                                        ALU.add).then_inc(res_done, 1)
                dve.wait_ge(res_done, c + 1)
                variance(c)
                if c > 0:
                    normalize_tokens(c - 1, B // 2 + c)
                    largest_tokens(c - 1)
            weights_low(2)
            normalize_tokens(B // 2 - 1, B)
            ins = largest_tokens(B // 2 - 1)
            link(ins)
            nc.vector.tensor_reduce(amax[0:TQ, 0:1], part[0:TQ, 0, 0:B // 2], AX.X, ALU.max).then_inc(amax_ready, 1)
            def scale_of(n, s_in):
                t, s, inv, f = (scl[:, n, c:c + 1] for c in range(4))
                dve.wait_ge(gmax_ready, n + 1)
                if s_in is None:
                    link(nc.vector.tensor_scalar(s, gmax[:, n:n + 1], 1.0 / ACT_QMAX, MIN_SCALE, ALU.mult, ALU.max))
                    nc.vector.reciprocal(inv, s).then_inc(scale_ready, 1)
                    return
                link(nc.vector.tensor_scalar(t, gmax[:, n:n + 1], s_in, 1.0 / ACT_QMAX, ALU.mult, ALU.mult))
                link(nc.vector.tensor_scalar(s, t, MIN_SCALE, None, ALU.max))
                link(nc.vector.reciprocal(inv, s))
                link(nc.vector.tensor_tensor(f, inv, s_in, ALU.mult))
                dve.sem_inc(scale_ready, 1)

            weights_low(3)
            scale_of(0, None)
            dve.wait_ge(scale_ready, 1)
            for c in range(B // 4, B // 2):
                dve.wait_ge(x_turned, c + 1)
                nc.vector.tensor_scalar(of_tokens(x_int, c), turned(c), scl[:, 0, 2:3], None, ALU.mult).then_inc(xint_dve, 1)
            for c in range(B // 2):
                dve.wait_ge(x_high, c + 1)
                nc.vector.tensor_tensor(of_tokens(xq[:, 1], c), of_tokens(x_int, c), of_tokens(xq[:, 0], c).bitcast(F32),
                                        ALU.subtract).then_inc(x_low, 1)
            for r in range(4, WGROUPS):
                weights_low(r)

            def largest_of_group(r):
                m, hf, fc = group(r)
                dve.wait_ge(gu_copied, r + 1)
                return nc.vector.tensor_reduce(part[:, 1 + m, hf * FC + fc:hf * FC + fc + 1],
                                               (gate, up)[m][:, fc, hf * HALF:(hf + 1) * HALF],
                                               AX.X, ALU.max, apply_absolute_value=True)

            def largest(n, pieces, ins):
                link(ins)
                nc.vector.tensor_reduce(amax[:, n:n + 1], part[:, n, 0:pieces], AX.X, ALU.max).then_inc(amax_ready, 1)

            for r in range(2 * FC):
                ins = largest_of_group(r)
            largest(1, 2 * FC, ins)
            scale_of(1, scl[:, 0, 1:2])
            for fc in range(FC):
                nc.vector.tensor_scalar(g_int[:, fc, :], gate[:, fc, :], scl[:, 1, 3:4], None, ALU.mult).then_inc(gint_done, 1)
            link(nc.vector.tensor_scalar(unit[:, 0:1], scl[:, 1, 1:2], 1.0 / UBITS, None, ALU.mult))
            largest_of_group(2 * FC)
            ins = largest_of_group(2 * FC + 1)
            for fc in range(FC + 1):
                if fc < FC:
                    dve.wait_ge(sint_done, fc + 1)
                    nc.vector.tensor_tensor(gate[:, fc, :], g_int[:, fc, :], s_int[:, fc, :], ALU.mult).then_inc(h_done, 1)
                if fc < FC - 1:
                    largest_of_group(2 * FC + 2 + 2 * fc)
                    ins = largest_of_group(2 * FC + 3 + 2 * fc)
                elif fc == FC - 1:
                    largest(2, 2 * FC, ins)
                if fc > 0:
                    dve.wait_ge(h_done, fc)
                    gated_max = nc.vector.tensor_reduce(part[:, 3, fc - 1:fc], gate[:, fc - 1, :], AX.X, ALU.max,
                                                        apply_absolute_value=True)
            largest(3, FC, gated_max)
            scale_of(2, scl[:, 0, 1:2])
            scale_of(3, unit[:, 0:1])
            link(nc.vector.tensor_scalar(g_int[:, 0, :], gate[:, 0, :], scl[:, 3, 3:4], None, ALU.mult))
            for fc in range(FC + 1):
                if fc < FC:
                    dve.wait_ge(uint_done, fc + 1)
                    if fc > 0:
                        dve.wait_ge(hint_done, fc)
                    nc.vector.tensor_tensor(up[:, fc, :], g_int[:, fc, :], u_int[:, fc, :], ALU.mult).then_inc(o_done, 1)
                if fc > 0:
                    dve.wait_ge(o_done, fc)
                    ins = nc.vector.tensor_reduce(part[:, 4, fc - 1:fc], up[:, fc - 1, :], AX.X, ALU.max,
                                                  apply_absolute_value=True)
            link(nc.vector.tensor_tensor(unit[:, 1:2], scl[:, 3, 1:2], scl[:, 2, 1:2], ALU.mult))
            largest(4, FC, ins)
            scale_of(4, unit[:, 1:2])
            for fc in range(FC):
                nc.vector.tensor_scalar(g_int[:, fc, :], up[:, fc, :], scl[:, 4, 3:4], None, ALU.mult).then_inc(oint_done, 1)
                dve.wait_ge(oint_done, fc + 1)
                nc.vector.tensor_copy(oq[0][:, fc, :], g_int[:, fc, :]).then_inc(o_high, 1)
                dve.wait_ge(o_high, fc + 1)
                nc.vector.tensor_tensor(oq[1][:, fc, :], g_int[:, fc, :], oq[0][:, fc, :].bitcast(F32), ALU.subtract).then_inc(o_low, 1)
            for b in range(B):
                dve.wait_ge(down_made, b + 1)
                nc.vector.scalar_tensor_tensor(out=x_sb[:, b, :], in0=bank[b][0:TQ, 0:DM], scalar=scl[0:TQ, 4, 1:2],
                                               in1=x_sb[:, b, :], op0=ALU.mult, op1=ALU.add).then_inc(y_done, 1)


def kernel(x, ctx_1024, mask_Bx1x1xS2_bk0, L0_xattn_Wq, L0_xattn_Wk, L0_xattn_Wv, L0_xattn_Wo, L0_xattn_rel_bias,
           L0_ffn_w_gate, L0_ffn_w_up, L0_ffn_w_down):
    import concourse.bacc as bacc
    from concourse.bass_utils import run_bass_kernel_spmd

    wq = np.asarray(L0_xattn_Wq).T.reshape(DM, NG, 1, GH * DK)
    onehot = np.zeros((NBUCKET, NREL), np.float32)
    for r in range(NREL):
        onehot[bucket_of(r - (TQ - 1)), r] = 1.0
    rows = np.arange(P) % (GH * DK) // DK
    padded = np.zeros((B, TKP, DM), np.float32)
    padded[:, :TK] = np.asarray(ctx_1024)
    layout = {
        "x": np.asarray(x)[:, ::-1].transpose(1, 0, 2),
        "ctxT": padded.reshape(B, TKP, KC, P).transpose(3, 0, 2, 1),
        "mask": np.asarray(mask_Bx1x1xS2_bk0).reshape(B, TK),
        "wqT": np.concatenate([wq, wq], axis=2).reshape(DM, NG, P),
        "wkT": np.asarray(L0_xattn_Wk).T,
        "wvT": np.asarray(L0_xattn_Wv).T,
        "woT": np.asarray(L0_xattn_Wo).T,
        "relT": np.asarray(L0_xattn_rel_bias).T,
        "w_gate": np.asarray(L0_ffn_w_gate),
        "w_up": np.asarray(L0_ffn_w_up),
        "w_down": np.asarray(L0_ffn_w_down),
        "onehot": onehot,
        "hmask": (rows[:, None] == np.arange(GH)[None, :]).astype(np.float32),
        "ident": np.eye(P, dtype=np.float32),
    }
    nc = bacc.Bacc("TRN2", target_bir_lowering=False, num_devices=1)
    arrays, args = {}, []
    for name, a in layout.items():
        a = np.ascontiguousarray(a)
        arrays[f"in_{name}"] = a
        args.append(nc.dram_tensor(f"in_{name}", a.shape, mybir.dt.from_np(a.dtype), kind="ExternalInput").ap())
    out = nc.dram_tensor("out_y", (TQ, B, DM), F32, kind="ExternalOutput").ap()
    build(nc, *args, out)
    r = run_bass_kernel_spmd(nc, [arrays], core_ids=[0])
    return np.ascontiguousarray(r.results[0]["out_y"].transpose(1, 0, 2)[:, ::-1])
```
